# Optimizing a Trainium2 kernel written in Bass

```python
import numpy as np
import jax
import jax.numpy as jnp

def _softmax(x, axis=-1):
    return jax.nn.softmax(x, axis=axis)

def _gelu(x):
    return jax.nn.gelu(x, approximate=True)

def _silu(x):
    return jax.nn.silu(x)

def _sigmoid(x):
    return jax.nn.sigmoid(x)

def _layernorm(x, axis=-1, eps=1e-05):
    m = jnp.mean(x, axis=axis, keepdims=True)
    v = jnp.var(x, axis=axis, keepdims=True)
    return (x - m) / jnp.sqrt(v + eps)

def _scatter_add(tgt, idx, src, axis=0):
    return tgt.at[idx].add(src)

def _segment_sum(src, seg, n):
    return jax.ops.segment_sum(src, seg, n)
kernel_name = 'mk_adaln_attn_ffn_d1_seqx_r8_6647e6'

def setup_inputs(seed: int=0):
    np.random.seed(seed)
    _w = jnp.asarray

    def _rec_inputs():
        import jax
        import jax.numpy as jnp
        _rk = jax.random.key(seed)
        x = -0.0003929 + 0.9999 * jax.random.normal(jax.random.fold_in(_rk, 1), (4, 256, 128), jnp.float32)
        _lenS = 256 - jax.random.randint(jax.random.fold_in(_rk, 7), (4,), 0, max(1, 256 // 4) + 1, jnp.int32)
        _lenS2 = 256 - jax.random.randint(jax.random.fold_in(_rk, 8), (4,), 0, max(1, 256 // 4) + 1, jnp.int32)
        fside_Bx1x1024x16_0 = 0.00222621 + 0.99962 * jax.random.normal(jax.random.fold_in(_rk, 11), (4, 1, 128, 16), jnp.float32)
        cond_1024 = -0.00745576 + 0.997402 * jax.random.normal(jax.random.fold_in(_rk, 12), (4, 128), jnp.float32)
        return (x, fside_Bx1x1024x16_0, cond_1024)
    x, fside_Bx1x1024x16_0, cond_1024 = _rec_inputs()

    def _L0_cond_setup():
        import jax, jax.numpy as jnp
        import numpy as np
        B, F_, IN, OUT, R = (32, 64, 128, 128, 16)
        key = jax.random.key(seed)
        ks = jax.random.split(key, 6)
        x = jax.random.normal(ks[0], (B, F_, IN), dtype=jnp.float32)
        u = jax.random.normal(ks[1], (B, 1, OUT, R), dtype=jnp.float32)
        v = jax.random.normal(ks[2], (B, 1, IN, R), dtype=jnp.float32)
        b = jax.random.normal(ks[3], (B, 1, OUT), dtype=jnp.float32)
        lim = 1.0 / np.sqrt(IN)
        W = jax.random.uniform(ks[4], (OUT, IN), minval=-lim, maxval=lim, dtype=jnp.float32)
        fc_bias = jax.random.uniform(ks[5], (OUT,), minval=-lim, maxval=lim, dtype=jnp.float32)
        return {'x': x, 'u': u, 'v': v, 'b': b, 'W': W, 'fc_bias': fc_bias}
    _L0_cond_all = _L0_cond_setup()
    _L0_cond_in = {k: v for k, v in _L0_cond_all.items() if k in ('W', 'fc_bias')}
    del _L0_cond_all

    def _L0_attn_setup():
        import jax, jax.numpy as jnp
        import numpy as np
        HEADS = 16
        DIM_HEAD = 64
        MAX_POS_EMB = 64
        SCALE = DIM_HEAD ** (-0.5)
        key = jax.random.key(seed)
        ks = jax.random.split(key, 6)
        B, T, D = (2, 256, 128)
        inner = HEADS * DIM_HEAD
        x = jax.random.normal(ks[0], (B, T, D), dtype=jnp.float32)
        Wq = jax.random.normal(ks[1], (D, inner), dtype=jnp.float32) * D ** (-0.5)
        Wkv = jax.random.normal(ks[2], (D, 2 * inner), dtype=jnp.float32) * D ** (-0.5)
        Wo = jax.random.normal(ks[3], (inner, D), dtype=jnp.float32) * inner ** (-0.5)
        bo = jnp.zeros((D,), dtype=jnp.float32)
        rel_emb = jax.random.normal(ks[4], (2 * MAX_POS_EMB + 1, DIM_HEAD), dtype=jnp.float32)
        return {'x': x, 'Wq': Wq, 'Wkv': Wkv, 'Wo': Wo, 'bo': bo, 'rel_emb': rel_emb}
    _L0_attn_all = _L0_attn_setup()
    _L0_attn_in = {k: v for k, v in _L0_attn_all.items() if k in ('Wq', 'Wkv', 'Wo', 'bo', 'rel_emb')}
    del _L0_attn_all

    def _L0_cond2_setup():
        import jax, jax.numpy as jnp
        import numpy as np
        B, T, D_IN, V_IN, E = (64, 128, 128, 128, 128)
        key = jax.random.key(seed)
        ks = jax.random.split(key, 16)
        s = 0.01
        return {'video': jax.random.normal(ks[0], (B, V_IN), jnp.float32), 'seq': jax.random.normal(ks[1], (B, T, D_IN), jnp.float32), 'W_z': jax.random.normal(ks[2], (D_IN, E), jnp.float32) * s, 'U_z': jax.random.normal(ks[3], (E, E), jnp.float32) * s, 'C_z': jax.random.normal(ks[4], (V_IN, E), jnp.float32) * s, 'b_z': jnp.zeros((E,), jnp.float32), 'W_r': jax.random.normal(ks[5], (D_IN, E), jnp.float32) * s, 'U_r': jax.random.normal(ks[6], (E, E), jnp.float32) * s, 'C_r': jax.random.normal(ks[7], (V_IN, E), jnp.float32) * s, 'b_r': jnp.zeros((E,), jnp.float32), 'W': jax.random.normal(ks[8], (D_IN, E), jnp.float32) * s, 'U': jax.random.normal(ks[9], (E, E), jnp.float32) * s, 'C': jax.random.normal(ks[10], (V_IN, E), jnp.float32) * s, 'b': jnp.zeros((E,), jnp.float32)}
    _L0_cond2_all = _L0_cond2_setup()
    _L0_cond2_in = {k: v for k, v in _L0_cond2_all.items() if k in ('W_z', 'U_z', 'C_z', 'b_z', 'W_r', 'U_r', 'C_r', 'b_r', 'W', 'U', 'C', 'b')}
    del _L0_cond2_all

    def _L0_ffn_setup():
        import jax, jax.numpy as jnp
        import numpy as np
        B, S, H, I, E = (2, 512, 128, 64, 8)
        key = jax.random.key(seed)
        ks = jax.random.split(key, 5)
        scale_h = 1.0 / np.sqrt(H)
        scale_i = 1.0 / np.sqrt(I)
        return {'hidden_states': jax.random.normal(ks[0], (B, S, H), dtype=jnp.float32), 'gate_w': jax.random.normal(ks[1], (E, H), dtype=jnp.float32) * scale_h, 'w_gate': jax.random.normal(ks[2], (E, I, H), dtype=jnp.float32) * scale_h, 'w_up': jax.random.normal(ks[3], (E, I, H), dtype=jnp.float32) * scale_h, 'w_down': jax.random.normal(ks[4], (E, H, I), dtype=jnp.float32) * scale_i}
    _L0_ffn_all = _L0_ffn_setup()
    _L0_ffn_in = {k: v for k, v in _L0_ffn_all.items() if k in ('gate_w', 'w_gate', 'w_up', 'w_down')}
    del _L0_ffn_all
    return {'x': x, 'fside_Bx1x1024x16_0': fside_Bx1x1024x16_0, 'cond_1024': cond_1024, 'L0_cond_W': _L0_cond_in['W'], 'L0_cond_fc_bias': _L0_cond_in['fc_bias'], 'L0_attn_Wq': _L0_attn_in['Wq'], 'L0_attn_Wkv': _L0_attn_in['Wkv'], 'L0_attn_Wo': _L0_attn_in['Wo'], 'L0_attn_bo': _L0_attn_in['bo'], 'L0_attn_rel_emb': _L0_attn_in['rel_emb'], 'L0_cond2_W_z': _L0_cond2_in['W_z'], 'L0_cond2_U_z': _L0_cond2_in['U_z'], 'L0_cond2_C_z': _L0_cond2_in['C_z'], 'L0_cond2_b_z': _L0_cond2_in['b_z'], 'L0_cond2_W_r': _L0_cond2_in['W_r'], 'L0_cond2_U_r': _L0_cond2_in['U_r'], 'L0_cond2_C_r': _L0_cond2_in['C_r'], 'L0_cond2_b_r': _L0_cond2_in['b_r'], 'L0_cond2_W': _L0_cond2_in['W'], 'L0_cond2_U': _L0_cond2_in['U'], 'L0_cond2_C': _L0_cond2_in['C'], 'L0_cond2_b': _L0_cond2_in['b'], 'L0_ffn_gate_w': _L0_ffn_in['gate_w'], 'L0_ffn_w_gate': _L0_ffn_in['w_gate'], 'L0_ffn_w_up': _L0_ffn_in['w_up'], 'L0_ffn_w_down': _L0_ffn_in['w_down']}

def reference(x, fside_Bx1x1024x16_0, cond_1024, L0_cond_W, L0_cond_fc_bias, L0_attn_Wq, L0_attn_Wkv, L0_attn_Wo, L0_attn_bo, L0_attn_rel_emb, L0_cond2_W_z, L0_cond2_U_z, L0_cond2_C_z, L0_cond2_b_z, L0_cond2_W_r, L0_cond2_U_r, L0_cond2_C_r, L0_cond2_b_r, L0_cond2_W, L0_cond2_U, L0_cond2_C, L0_cond2_b, L0_ffn_gate_w, L0_ffn_w_gate, L0_ffn_w_up, L0_ffn_w_down):
    import jax
    import jax.numpy as jnp

    def _L0_cond_ref(x, u, v, b, W, fc_bias):
        import jax, jax.numpy as jnp
        import numpy as np
        B, F_, IN, OUT, R = (32, 64, 128, 128, 16)
        inch = x.shape[-1]
        r = v.shape[-1]
        z1 = jnp.einsum('bfi,bir->bfr', x, v[:, 0]) / inch
        z = jnp.einsum('bfr,bor->bfo', z1, u[:, 0]) / r
        y = jnp.einsum('bfi,oi->bfo', x, W) + fc_bias + z + b
        return jax.nn.gelu(y, approximate=False)

    def _L0_attn_ref(x, Wq, Wkv, Wo, bo, rel_emb):
        import jax, jax.numpy as jnp
        import numpy as np
        HEADS = 16
        DIM_HEAD = 64
        MAX_POS_EMB = 64
        SCALE = DIM_HEAD ** (-0.5)
        B, T, D = x.shape
        h, d = (HEADS, DIM_HEAD)
        q = (x @ Wq).reshape(B, T, h, d).transpose(0, 2, 1, 3)
        kv = x @ Wkv
        k, v = jnp.split(kv, 2, axis=-1)
        k = k.reshape(B, T, h, d).transpose(0, 2, 1, 3)
        v = v.reshape(B, T, h, d).transpose(0, 2, 1, 3)
        dots = jnp.einsum('bhid,bhjd->bhij', q, k) * SCALE
        seq = jnp.arange(T)
        dist = jnp.clip(seq[:, None] - seq[None, :], -MAX_POS_EMB, MAX_POS_EMB) + MAX_POS_EMB
        rpe = rel_emb[dist]
        pos_attn = jnp.einsum('bhnd,nrd->bhnr', q, rpe) * SCALE
        attn = jax.nn.softmax(dots + pos_attn, axis=-1)
        out = jnp.einsum('bhij,bhjd->bhid', attn, v)
        out = out.transpose(0, 2, 1, 3).reshape(B, T, h * d)
        return out @ Wo + bo

    def _L0_cond2_ref(video, seq, W_z, U_z, C_z, b_z, W_r, U_r, C_r, b_r, W, U, C, b):
        import jax, jax.numpy as jnp
        import numpy as np
        B, T, D_IN, V_IN, E = (64, 128, 128, 128, 128)
        vz = video @ C_z + b_z
        vr = video @ C_r + b_r
        vh = video @ C + b
        xz = jnp.einsum('btd,de->bte', seq, W_z)
        xr = jnp.einsum('btd,de->bte', seq, W_r)
        xh = jnp.einsum('btd,de->bte', seq, W)

        def step(h, xs):
            xzt, xrt, xht = xs
            z = jax.nn.sigmoid(xzt + h @ U_z + vz)
            r = jax.nn.sigmoid(xrt + h @ U_r + vr)
            hh = jnp.tanh(xht + r * h @ U + vh)
            h_new = (1.0 - z) * h + z * hh
            return (h_new, h_new)
        h0 = jnp.zeros((seq.shape[0], U.shape[0]), seq.dtype)
        xs = (jnp.swapaxes(xz, 0, 1), jnp.swapaxes(xr, 0, 1), jnp.swapaxes(xh, 0, 1))
        _, out_t = jax.lax.scan(step, h0, xs)
        return jnp.swapaxes(out_t, 0, 1)

    def _L0_ffn_ref(hidden_states, gate_w, w_gate, w_up, w_down):
        import jax, jax.numpy as jnp
        import numpy as np
        B, S, H, I, E = (2, 512, 128, 64, 8)
        b, s, h = hidden_states.shape
        x = hidden_states.reshape(-1, h)
        logits = x @ gate_w.T
        top_v = jnp.max(logits, axis=-1)
        sel = jnp.argmax(logits, axis=-1)
        rw = jax.nn.sigmoid(top_v)
        out = jnp.zeros_like(x)
        n_exp = gate_w.shape[0]
        for e in range(n_exp):
            mask = (sel == e).astype(x.dtype)
            xs = x * (rw * mask)[:, None]
            g = xs @ w_gate[e].T
            u = xs @ w_up[e].T
            out = out + u * jax.nn.silu(g) @ w_down[e].T
        return out.reshape(b, s, h)
    x = x + _L0_attn_ref(_L0_cond_ref(x, fside_Bx1x1024x16_0, fside_Bx1x1024x16_0, cond_1024[:, None, :], L0_cond_W, L0_cond_fc_bias), L0_attn_Wq, L0_attn_Wkv, L0_attn_Wo, L0_attn_bo, L0_attn_rel_emb)
    x = x + _L0_ffn_ref(_L0_cond2_ref(cond_1024, x, L0_cond2_W_z, L0_cond2_U_z, L0_cond2_C_z, L0_cond2_b_z, L0_cond2_W_r, L0_cond2_U_r, L0_cond2_C_r, L0_cond2_b_r, L0_cond2_W, L0_cond2_U, L0_cond2_C, L0_cond2_b), L0_ffn_gate_w, L0_ffn_w_gate, L0_ffn_w_up, L0_ffn_w_down)
    return x

_drawn_inputs = setup_inputs


def setup_inputs(seed=0):
    import zlib

    import numpy as np

    out = dict(_drawn_inputs(seed))
    spreads = {'L0_attn_bo': (0.0, 0.1),
     'L0_cond2_b_z': (0.0, 0.8),
     'L0_cond2_b_r': (0.0, 0.8),
     'L0_cond2_b': (0.0, 0.8)}
    factors = {'fside_Bx1x1024x16_0': 8.0,
     'L0_attn_rel_emb': 3.161,
     'L0_cond2_W_z': 8.0,
     'L0_cond2_U_z': 8.0,
     'L0_cond2_C_z': 8.0,
     'L0_cond2_W_r': 8.0,
     'L0_cond2_U_r': 8.0,
     'L0_cond2_C_r': 8.0,
     'L0_cond2_W': 8.0,
     'L0_cond2_U': 8.0,
     'L0_cond2_C': 8.0,
     'L0_ffn_gate_w': 8.0,
     'L0_ffn_w_gate': 8.0,
     'L0_ffn_w_up': 8.0,
     'L0_ffn_w_down': 8.0}
    for name, (base, spread) in spreads.items():
        noise = np.random.default_rng([zlib.crc32(name.encode()), seed]).standard_normal(out[name].shape)
        drawn = base * np.exp(spread * noise) if base else spread * noise
        out[name] = jnp.asarray(drawn.astype(out[name].dtype))
    for name, factor in factors.items():
        out[name] = (out[name] * factor).astype(out[name].dtype)
    return out
```

```python
from contextlib import ExitStack

import concourse.bass as bass
from concourse import mybir

F32 = mybir.dt.float32
F16 = mybir.dt.float16
BF16 = mybir.dt.bfloat16
U32 = mybir.dt.uint32
ALU = mybir.AluOpType
ACT = mybir.ActivationFunctionType
AX_X = mybir.AxisListType.X

B, T, D = 4, 256, 128
RANK = 16
HEADS, DH = 16, 64
PAIRS = HEADS // 2
INNER = HEADS * DH
POS = 64
CH = 64
NCH = T // CH
GROUPS = NCH * B
RW = 2 * T - 1
EW = T + CH - 1
SCALE = DH ** -0.5
EXPERTS, HID = 8, 64
LOWEST = 3.0e38
SPLIT = 4096.0
UNROLL = 8
TOK = 128
STEPS_TILE = TOK // B


def build(nc, x, side, cond, w_cond, fc_bias, wq, wkv, wo, bo, rel,
          w_z, u_z, c_z, b_z, w_r, u_r, c_r, b_r, w_c, u_c, c_c, b_c,
          gate_w, w_gate, w_up, w_down, out):
    with ExitStack() as ctx:
        def sb(name, shape, dt=F32):
            return ctx.enter_context(nc.sbuf_tensor(name, shape, dt))

        def sem(name):
            return ctx.enter_context(nc.semaphore(name))

        bank = [ctx.enter_context(nc.psum_tensor(f"bank{i}", [128, 512], F32)) for i in range(8)]
        skew = nc.dram_tensor("skew", (PAIRS, 128, EW), F32, kind="Internal").ap()

        ident = sb("ident", [128, 128])
        flip = sb("flip", [128, 128])
        ones4 = sb("ones4", [128, 4])
        x_nat = sb("x_nat", [128, B * T // 128, D])
        f_nat = sb("f_nat", [128, B, RANK])
        cond_nat = sb("cond_nat", [B, D])
        w_nat = sb("w_nat", [128, D])
        rel_nat = sb("rel_nat", [128, 2, DH])
        rel_end = sb("rel_end", [128, 2])
        cols = sb("cols", [128, 5])
        wq_sb = sb("wq_sb", [128, INNER])
        wkv_sb = sb("wkv_sb", [128, 2 * INNER])
        wo_sb = sb("wo_sb", [128, PAIRS, D])
        wx = sb("wx", [128, 3, D])
        wu = sb("wu", [128, 3, D])
        wc = sb("wc", [128, 3, D])
        gate_nat = sb("gate_nat", [EXPERTS, D])
        ffn_nat = sb("ffn_nat", [128, 3, 512])
        xT = sb("xT", [128, B * T])
        wT = sb("wT", [128, D])
        condT = sb("condT", [128, B])
        ybias = sb("ybias", [128, B])
        fT = sb("fT", [RANK, B, 128])
        mix = sb("mix", [128, B, D])
        yT = sb("yT", [128, B * T])
        kT = sb("kT", [128, B, PAIRS, T])
        qT = sb("qT", [128, NCH, B, PAIRS, CH])
        v_sb = sb("v_sb", [128, B, PAIRS, 2, 128])
        rext = sb("rext", [128, RW + 1])
        vbias = sb("vbias", [128, 3, B])
        ffnT = sb("ffnT", [128, 3, 512])
        gateT = sb("gateT", [128, EXPERTS])
        qa = sb("qa", [128, 2, 128])
        qb = sb("qb", [128, 2, 128])
        e_sb = sb("e_sb", [128, 4, EW])
        pos = sb("pos", [128, PAIRS, T])
        s_sb = sb("s_sb", [128, 2, T])
        p_sb = sb("p_sb", [128, 2, T])
        pt_sb = sb("pt_sb", [128, 2, T])
        nmax = sb("nmax", [128, PAIRS])
        rsum = sb("rsum", [128, PAIRS])
        rinv = sb("rinv", [128, PAIRS])
        o_sb = sb("o_sb", [128, PAIRS, DH])
        oT = sb("oT", [128, PAIRS, CH])
        x1T = sb("x1T", [128, T, B])
        up32 = sb("up32", [128, D])
        parts = sb("parts", [128, 3, 3, D], BF16)
        uw = sb("uw", [128, 3, 2, 2, 3, D], BF16)
        st = {n: sb(n, [128, 2, B], dt) for n, dt in (
            ("tr", F32), ("tz", F32), ("hh", F32), ("d", F32), ("d8", F32), ("q1", F16), ("q8", F32), ("q2", F16),
            ("b1", F16), ("b8", F32), ("b2", F16), ("z8", F32), ("g1", F16), ("g8", F32), ("g2", F16))}
        hist = x_nat[:, :, :].rearrange("p a d -> p (a d)").rearrange("p (t b) -> p t b", b=B)
        hs = sb("hs", [128, B, STEPS_TILE])
        xs = sb("xs", [128, B, STEPS_TILE])
        lg = sb("lg", [128, EXPERTS])
        top = sb("top", [128, 8])
        idx = sb("idx", [128, 8], U32)
        idxf = sb("idxf", [128, 1])
        rw = sb("rw", [128, 1])
        rw2 = sb("rw2", [128, 1])
        pad = sb("pad", [128, 4])
        hist_pad = sb("hist_pad", [128, 1])
        iota = sb("iota", [128, EXPERTS])
        mask = sb("mask", [128, EXPERTS])
        gm = sb("gm", [128, EXPERTS, HID])
        um = sb("um", [128, EXPERTS, HID])
        th = sb("th", [128, EXPERTS, HID])
        sg, act_h = th, um
        aT = sb("aT", [128, 4, 128])
        y_out = sb("y_out", [128, D])

        ld = {n: sem(f"ld_{n}") for n in ("x", "cond", "rel", "w", "att", "gru", "ffn")}
        consts = sem("consts")
        setup_pe = sem("setup_pe")
        setup_act = sem("setup_act")
        setup_dve = sem("setup_dve")
        dve_self = sem("dve_self")
        kqv_pe, kqv_act, kqv_dve = sem("kqv_pe"), sem("kqv_act"), sem("kqv_dve")
        qa_ready, qb_ready = sem("qa_ready"), sem("qb_ready")
        qr_done, e_ready = sem("qr_done"), sem("e_ready")
        e_stored = [sem(f"e_stored{u}") for u in range(PAIRS)]
        pos_in = [sem(f"pos_in{u}") for u in range(PAIRS)]
        qk_done, s_ready, p_ready = sem("qk_done"), sem("s_ready"), sem("p_ready")
        t_done, pt_ready, pv_done, o_ready = sem("t_done"), sem("pt_ready"), sem("pv_done"), sem("o_ready")
        rinv_ready = sem("rinv_ready")
        ot_done, oT_ready, wo_done, x1_ready = sem("ot_done"), sem("oT_ready"), sem("wo_done"), sem("x1_ready")
        u_self = sem("u_self")
        gru_init = sem("gru_init")
        xp_done = sem("xp_done")
        r_pre, z_pre, c_pre = sem("r_pre"), sem("z_pre"), sem("c_pre")
        tr_ok, tz_ok, hh_ok = sem("tr_ok"), sem("tz_ok"), sem("hh_ok")
        q1_ok, q8_ok, q2_ok = sem("q1_ok"), sem("q8_ok"), sem("q2_ok")
        b1_ok, b8_ok, b2_ok, z8_ok = sem("b1_ok"), sem("b8_ok"), sem("b2_ok"), sem("z8_ok")
        g1_ok, g8_ok, g2_ok, d8_ok, d_ok = sem("g1_ok"), sem("g8_ok"), sem("g2_ok"), sem("d8_ok"), sem("d_ok")
        hist_ok = sem("hist_ok")
        hs_ok, lg_done, gu_done, th_ok = sem("hs_ok"), sem("lg_done"), sem("gu_done"), sem("th_ok")
        rwt_ok, fdve, at_done, aT_ok, y_done, y_ok = (sem("rwt_ok"), sem("fdve"), sem("at_done"), sem("aT_ok"),
                                                      sem("y_done"), sem("y_ok"))
        act_free = sem("act_free")
        stored = sem("stored")

        block = ctx.enter_context(nc.Block())
        col = lambda v: v.rearrange("(p a) -> p a", a=1)

        def kqv_out(item, src, copy):
            kind, a, s = item
            if kind == "k":
                return copy(kT[:, 2 * s:2 * s + 2, a, :], src[:, :].rearrange("p (b n) -> p b n", b=2))
            if kind == "q":
                return copy(qT[:, :, 2 * s:2 * s + 2, a, :], src[:, :].rearrange("p (b c n) -> p c b n", b=2, c=NCH))
            return copy(v_sb[:, a // 2, 4 * s:4 * s + 4, a % 2, :], src[:, :].rearrange("p (h d) -> p h d", h=4))

        @block.sync
        def _(sp):
            sp.dma_start(x_nat[:, :, :], x.rearrange("b (a p) d -> p (b a) d", p=128)).then_inc(ld["x"], 16)
            sp.dma_start(f_nat[:, :, :], side.rearrange("b a p r -> p (b a) r")).then_inc(ld["cond"], 16)
            sp.dma_start(cond_nat[:, :], cond).then_inc(ld["cond"], 16)
            sp.dma_start(w_nat[:, :], w_cond).then_inc(ld["cond"], 16)
            for k, vec in enumerate((fc_bias, bo, b_r, b_z, b_c)):
                sp.dma_start(cols[:, k:k + 1], col(vec)).then_inc(ld["cond"], 16)
            for e in range(2):
                sp.dma_start(rel_nat[:, e, :], rel[0:128, :]).then_inc(ld["rel"], 16)
                sp.dma_start(rel_end[e * DH:(e + 1) * DH, 0:1], rel[2 * POS:2 * POS + 1, :].rearrange("a d -> d a")).then_inc(ld["rel"], 16)
                sp.dma_start(rel_end[e * DH:(e + 1) * DH, 1:2], rel[0:1, :].rearrange("a d -> d a")).then_inc(ld["rel"], 16)

            def skew_unit(g, u):
                sp.wait_ge(e_ready, g * PAIRS + u + 1)
                sp.dma_start(skew[u], e_sb[:, u % 4, :]).then_inc(e_stored[u], 16)

            def unskew_unit(g, u):
                sp.wait_ge(e_stored[u], g * 16 + 16)
                for e in range(2):
                    src = skew[u, e * CH:(e + 1) * CH, :].copy()
                    src = bass.AP(tensor=src.tensor, offset=src.offset + CH - 1, ap=[[EW - 1, CH], [1, T]])
                    sp.dma_start(pos[e * CH:(e + 1) * CH, u, :], src).then_inc(pos_in[u], 16)

            def skew_group(g):
                for u in range(PAIRS + 1):
                    if u < PAIRS:
                        skew_unit(g, u)
                    if u:
                        unskew_unit(g, u - 1)

            skew_group(0)
            with sp.Fori(0, GROUPS - 1) as i:
                skew_group(i + 1)

            with sp.Fori(0, B * T // TOK) as i:
                row = sp.snap(i * STEPS_TILE)
                sp.wait_ge(y_ok, i + 1)
                for b in range(B):
                    sp.dma_start(out[b, bass.ds(row, STEPS_TILE), :],
                                 y_out[b * STEPS_TILE:(b + 1) * STEPS_TILE, :]).then_inc(stored, 16)
            sp.wait_ge(stored, 16 * B * B * T // TOK)

        @block.gpsimd
        def _(pool):
            pool.memset(ident[:, :], 0.0).then_inc(consts, 1)
            pool.memset(flip[:, :], 0.0).then_inc(consts, 1)
            pool.memset(qa[:, :, :], 0.0).then_inc(consts, 1)
            pool.memset(qb[:, :, :], 0.0).then_inc(consts, 1)
            for e in range(EXPERTS):
                pool.memset(iota[:, e:e + 1], float(e))
            pool.memset(rext[:, :], 0.0).then_inc(consts, 1)
            pool.memset(hist_pad[:, :], 0.0).then_inc(hist_ok, 2)
            pool.wait_ge(consts, 5)
            pool.affine_select(out=ident[:, :], in_=ident[:, :], compare_op=ALU.not_equal, fill=1.0,
                               base=0, pattern=[[-1, 128]], channel_multiplier=1).then_inc(consts, 1)
            pool.affine_select(out=flip[:, :], in_=flip[:, :], compare_op=ALU.not_equal, fill=1.0,
                               base=-127, pattern=[[1, 128]], channel_multiplier=1).then_inc(consts, 1)

            def stage(dst, ready, used, g, u, first):
                n = g * PAIRS + u
                if not (first and u < 2):
                    pool.wait_ge(used, n - 1)
                for e in range(2):
                    h = slice(e * DH, (e + 1) * DH)
                    ins = pool.tensor_copy(dst[h, u % 2, e * CH:(e + 1) * CH], qT2[h, bass.ds(n * CH, CH)])
                ins.then_inc(ready, 1)

            qT2 = qT[:, :, :, :, :].rearrange("p c b h n -> p (c b h n)")
            pool.wait_ge(kqv_act, KQV_ACT)
            pool.wait_ge(kqv_dve, KQV_DVE)
            for u in range(PAIRS):
                stage(qa, qa_ready, qr_done, 0, u, True)

            def both(i, u):
                stage(qa, qa_ready, qr_done, i + 1, u, False)

            for u in range(PAIRS):
                both(0, u)
                stage(qb, qb_ready, qk_done, 0, u, True)
            with pool.Fori(1, GROUPS - 1) as i:
                for u in range(PAIRS):
                    both(i, u)
                    stage(qb, qb_ready, qk_done, i, u, False)
            for u in range(PAIRS):
                stage(qb, qb_ready, qk_done, GROUPS - 1, u, False)

            with pool.Fori(0, T // UNROLL) as i:
                for k in range(UNROLL):
                    pool.wait_ge(d_ok, i * UNROLL + k + 2)
                    pool.tensor_copy(hist[:, bass.ds(i * UNROLL + k, 1), :], st["d"][:, k % 2:k % 2 + 1, :]).then_inc(hist_ok, 1)

        @block.tensor
        def _(pe):
            mm = pe.matmul
            pe.wait_ge(consts, 7)
            pe.wait_ge(ld["x"], 16)
            for s in range(2):
                for k in range(4):
                    ins = pe.transpose(bank[s][:, k * 128:(k + 1) * 128], x_nat[:, s * 4 + k, :], ident[:, :])
                ins.then_inc(setup_pe, 1)
            pe.wait_ge(ld["cond"], 128)
            pe.transpose(bank[2][:, 0:128], w_nat[:, :], ident[:, :])
            pe.transpose(bank[2][:, 128:128 + B], cond_nat[:, :], ident[0:B, 0:B]).then_inc(setup_pe, 1)
            for b in range(B):
                ins = pe.transpose(bank[3][0:RANK, b * 128:(b + 1) * 128], f_nat[:, b, :], ident[:, :])
            ins.then_inc(setup_pe, 1)
            pe.wait_ge(ld["rel"], 96)
            pe.transpose(bank[4][:, 0:128], rel_nat[:, :, :].rearrange("p a d -> p (a d)"), flip[:, :]).then_inc(setup_pe, 1)
            pe.wait_ge(setup_act, 2)
            for b in range(B):
                ins = mm(bank[5][:, b * 128:(b + 1) * 128], fT[:, b, :], fT[:, b, :], start=True, stop=True)
            ins.then_inc(setup_pe, 1)
            pe.wait_ge(setup_dve, 5)
            pe.wait_ge(setup_act, 3)
            for b in range(B):
                mm(bank[7 - b][:, 0:T], mix[:, b, :], xT[:, b * T:(b + 1) * T],
                   start=True, stop=True).then_inc(setup_pe, 1)
            pe.wait_ge(ld["ffn"], 64)
            for j in range(3):
                for k in range(4):
                    ins = pe.transpose(bank[j][:, k * 128:(k + 1) * 128], ffn_nat[:, j, k * 128:(k + 1) * 128], ident[:, :])
                ins.then_inc(setup_pe, 1)
            pe.wait_ge(ld["gru"], 144)
            pe.transpose(bank[3][:, 0:EXPERTS], gate_nat[:, :], ident[0:EXPERTS, 0:EXPERTS])
            for k in range(3):
                ins = mm(bank[3][:, 16 + 4 * k:20 + 4 * k], wc[:, k, :], condT[:, :], start=True, stop=True)
            ins.then_inc(setup_pe, 1)

            pe.wait_ge(ld["att"], 48)
            pe.wait_ge(setup_act, 7)
            pe.wait_ge(setup_dve, SETUP_DVE)
            pe.wait_ge(setup_act, SETUP_ACT)
            for n, (kind, a, s) in enumerate(KQV):
                if n >= 8:
                    pe.wait_ge(*((kqv_act, n // 2 - 3) if n % 2 == 0 else (kqv_dve, (n - 1) // 2 - 3)))
                half = slice(s * 512, (s + 1) * 512)
                if kind == "k":
                    ins = mm(bank[n % 8][:, :], wkv_sb[:, a * 128:(a + 1) * 128], yT[:, half], start=True, stop=True)
                elif kind == "q":
                    ins = mm(bank[n % 8][:, :], wq_sb[:, a * 128:(a + 1) * 128], yT[:, half], start=True, stop=True)
                else:
                    ins = mm(bank[n % 8][:, :], yT[:, a * 128:(a + 1) * 128], wkv_sb[:, INNER + s * 512:INNER + (s + 1) * 512],
                             start=True, stop=True)
                ins.then_inc(kqv_pe, 1)

            kT2 = kT[:, :, :, :].rearrange("p b h n -> p (b h n)")
            v2 = v_sb[:, :, :, :, :].rearrange("p b h r d -> p (b h r d)")

            def positions(g, u, first):
                n = g * PAIRS + u
                pe.wait_ge(qa_ready, n + 1)
                if not (first and u < 2):
                    pe.wait_ge(e_ready, n - 1)
                mm(bank[u % 2][:, 0:EW], qa[:, u % 2, :], rext[:, bass.ds(T - CH - (g // B) * CH, EW)],
                   start=True, stop=True).then_inc(qr_done, 1)

            def scores(g, u, first):
                n = g * PAIRS + u
                pe.wait_ge(qb_ready, n + 1)
                if not (first and u < 2):
                    pe.wait_ge(s_ready, n - 1)
                mm(bank[2 + u % 2][:, 0:T], qb[:, u % 2, :], kT2[:, bass.ds(((g % B) * PAIRS + u) * T, T)],
                   start=True, stop=True).then_inc(qk_done, 1)

            def transpose_p(g, u, first):
                n = g * PAIRS + u
                pe.wait_ge(p_ready, n + 1)
                if not (first and u < 2):
                    pe.wait_ge(o_ready, n - 1)
                for r in range(2):
                    ins = pe.transpose(bank[4 + u % 2][:, r * 128:(r + 1) * 128], p_sb[:, u % 2, r * 128:(r + 1) * 128], ident[:, :])
                ins.then_inc(t_done, 1)

            def values(g, u):
                n = g * PAIRS + u
                pe.wait_ge(pt_ready, n + 1)
                for r in range(2):
                    ins = mm(bank[4 + u % 2][:, T:T + 128], pt_sb[:, u % 2, r * 128:(r + 1) * 128],
                             v2[:, bass.ds((((g % B) * PAIRS + u) * 2 + r) * 128, 128)], start=(r == 0), stop=(r == 1))
                ins.then_inc(pv_done, 1)

            def project(g):
                pe.wait_ge(o_ready, g * PAIRS + PAIRS)
                for u in range(0, PAIRS, 2):
                    ins = pe.transpose(bank[6][:, u * 64:u * 64 + 128], o_sb[:, u:u + 2, :].rearrange("p u d -> p (u d)"), ident[:, :])
                ins.then_inc(ot_done, 1)
                pe.wait_ge(oT_ready, g * 4 + 4)
                for u in range(PAIRS):
                    ins = mm(bank[7][:, 0:CH], wo_sb[:, u, :], oT[:, u, :], start=(u == 0), stop=(u == PAIRS - 1))
                ins.then_inc(wo_done, 1)

            def group(g, ahead, first):
                for u in range(PAIRS + 2):
                    if u < PAIRS:
                        if ahead:
                            positions(g + 1, u, False)
                        scores(g, u, first)
                    if 1 <= u <= PAIRS:
                        transpose_p(g, u - 1, first)
                    if u >= 2:
                        values(g, u - 2)
                if not first:
                    pe.wait_ge(x1_ready, g)
                project(g)

            pe.wait_ge(kqv_act, KQV_ACT)
            pe.wait_ge(kqv_dve, KQV_DVE)
            for u in range(PAIRS):
                positions(0, u, True)
            group(0, True, True)
            with pe.Fori(1, GROUPS - 1) as i:
                group(i, True, False)
            group(GROUPS - 1, False, False)

            x1f = x1T[:, :, :].rearrange("p t b -> p (t b)")
            pe.wait_ge(x1_ready, GROUPS)
            pe.wait_ge(gru_init, 6)
            with pe.Fori(0, 2) as c:
                pe.wait_ge(g1_ok, c * 128 + 1)
                for k in range(3):
                    mm(bank[k][:, :], wx[:, k, :], x1f[:, bass.ds(c * 512, 512)], start=True, stop=True)
                    mm(bank[k][:, :], ident[:, :], vbias[:, k:k + 1, :].broadcast_to([128, 128, B]), start=False, stop=True,
                       skip_group_check=True)
                with pe.Fori(0, 128 // UNROLL) as i:
                    for k in range(UNROLL):
                        t = c * 128 + i * UNROLL + k
                        w = bass.ds((i * UNROLL + k) * B, B)
                        now, before = k % 2, 1 - k % 2

                        def product(gate, use, low, operand):
                            for j in range(3):
                                last = mm(bank[gate][:, w], uw[:, gate, use, low, j, :], operand, start=False, stop=True,
                                          skip_group_check=True)
                            return last

                        pe.wait_ge(b1_ok, t + 1)
                        product(0, 1, 0, st["b1"][:, before, :])
                        product(1, 1, 0, st["b1"][:, before, :])
                        pe.wait_ge(b2_ok, t + 1)
                        product(0, 1, 1, st["b2"][:, before, :])
                        product(1, 1, 1, st["b2"][:, before, :])
                        pe.wait_ge(g1_ok, t + 1)
                        product(0, 0, 0, st["g1"][:, before, :])
                        product(1, 0, 0, st["g1"][:, before, :])
                        pe.wait_ge(g2_ok, t + 1)
                        product(0, 0, 1, st["g2"][:, before, :]).then_inc(r_pre, 1)
                        product(1, 0, 1, st["g2"][:, before, :]).then_inc(z_pre, 1)
                        pe.wait_ge(q1_ok, t + 1)
                        product(2, 0, 0, st["q1"][:, now, :])
                        pe.wait_ge(q2_ok, t + 1)
                        product(2, 0, 1, st["q2"][:, now, :]).then_inc(c_pre, 1)

            pe.wait_ge(hh_ok, T)
            def tile(i, first):
                hflat = hs[:, :, :].rearrange("p b t -> p (b t)")
                pe.wait_ge(hs_ok, i + 1)
                if not first:
                    pe.wait_ge(fdve, i * FD)
                mm(bank[3][:, 0:EXPERTS], hflat, gateT[:, :], start=True, stop=True).then_inc(lg_done, 1)
                mm(bank[4][:, :], hflat, ffnT[:, 0, :], start=True, stop=True).then_inc(gu_done, 1)
                mm(bank[5][:, :], hflat, ffnT[:, 1, :], start=True, stop=True).then_inc(gu_done, 1)
                mm(bank[6][:, 0:D], xs[:, :, :].rearrange("p b t -> p (b t)"), ident[:, :], start=True, stop=False)
                pe.wait_ge(fdve, i * FD + FD - 1)
                for k in range(4):
                    ins = pe.transpose(bank[7][:, k * 128:(k + 1) * 128],
                                       act_h[:, 2 * k:2 * k + 2, :].rearrange("p e n -> p (e n)"), ident[:, :])
                ins.then_inc(at_done, 1)
                pe.wait_ge(aT_ok, i + 1)
                for k in range(4):
                    ins = mm(bank[6][:, 0:D], aT[:, k, :], ffnT[:, 2, k * 128:(k + 1) * 128], start=False, stop=(k == 3))
                ins.then_inc(y_done, 1)

            tile(0, True)
            with pe.Fori(1, B * T // TOK) as i:
                tile(i, False)

        @block.scalar
        def _(act):
            act.dma_start(wkv_sb[:, :], wkv).then_inc(ld["att"], 16)
            act.dma_start(wq_sb[:, :], wq).then_inc(ld["att"], 16)
            act.dma_start(wo_sb[:, :, :], wo.rearrange("(u p) d -> p u d", p=128)).then_inc(ld["att"], 16)
            for k, (w_, u_, c_) in enumerate(((w_r, u_r, c_r), (w_z, u_z, c_z), (w_c, u_c, c_c))):
                act.dma_start(wx[:, k, :], w_).then_inc(ld["gru"], 16)
                act.dma_start(wu[:, k, :], u_).then_inc(ld["gru"], 16)
                act.dma_start(wc[:, k, :], c_).then_inc(ld["gru"], 16)
            act.dma_start(gate_nat[:, :], gate_w).then_inc(ld["ffn"], 16)
            for j, w_ in enumerate((w_gate, w_up)):
                act.dma_start(ffn_nat[:, j, :].rearrange("p (a d) -> p a d", a=4),
                              w_.rearrange("e n d -> (e n) d").rearrange("(a p) d -> p a d", p=128)).then_inc(ld["ffn"], 16)
            act.dma_start(ffn_nat[:, 2, :].rearrange("p (e n) -> p e n", e=EXPERTS),
                          w_down.rearrange("e d n -> d e n")).then_inc(ld["ffn"], 16)
            cp = lambda o, i: act.activation(o, i, ACT.Copy)
            act.wait_ge(setup_pe, 3)
            cp(wT[:, :], bank[2][:, 0:128]).then_inc(setup_act, 1)
            act.wait_ge(setup_pe, 4)
            cp(fT[:, :, :].rearrange("p b n -> p (b n)"), bank[3][0:RANK, :]).then_inc(setup_act, 1)
            act.wait_ge(setup_pe, 5)
            cp(rext[:, T - POS:T + POS], bank[4][:, 0:128]).then_inc(setup_act, 1)
            act.wait_ge(setup_dve, 3)
            for b in range(B):
                act.wait_ge(setup_pe, 7 + b)
                act.activation(yT[:, b * T:(b + 1) * T], bank[7 - b][:, 0:T], ACT.Gelu,
                               bias=ybias[:, b:b + 1]).then_inc(setup_act, 1)
            for j in range(3):
                act.wait_ge(setup_pe, 11 + j)
                cp(ffnT[:, j, :], bank[j][:, :]).then_inc(setup_act, 1)

            for n, item in enumerate(KQV):
                if n % 2 == 0:
                    act.wait_ge(kqv_pe, n + 1)
                    kqv_out(item, bank[n % 8], cp).then_inc(kqv_act, 1)

            def move_e(g, u, first):
                n = g * PAIRS + u
                act.wait_ge(qr_done, n + 1)
                if not (first and u < 4):
                    act.wait_ge(e_stored[(u - 4) % PAIRS], 16 * g + (16 if u >= 4 else 0))
                cp(e_sb[:, u % 4, :], bank[u % 2][:, 0:EW]).then_inc(e_ready, 1)

            def exps(g, u, first):
                n = g * PAIRS + u
                act.wait_ge(s_ready, n + 1)
                if not (first and u < 2):
                    act.wait_ge(t_done, n - 1)
                act.activation(p_sb[:, u % 2, :], s_sb[:, u % 2, :], ACT.Exp, bias=nmax[:, u:u + 1], scale=-1.0,
                               accum_out=rsum[:, u:u + 1]).then_inc(p_ready, 1)

            def project(g):
                act.wait_ge(ot_done, g + 1)
                for odd in range(2):
                    for e in range(2):
                        cp(oT[e * DH:(e + 1) * DH, odd::2, :],
                           bank[6][odd * DH:(odd + 1) * DH, :].rearrange("p (u n) -> p u n", u=4)[:, :, e * CH:(e + 1) * CH]).then_inc(oT_ready, 1)

            def group(g, ahead, first):
                for u in range(PAIRS):
                    exps(g, u, first)
                    if ahead:
                        move_e(g + 1, u, False)
                project(g)

            for u in range(PAIRS):
                move_e(0, u, True)
            group(0, True, True)
            with act.Fori(1, GROUPS - 1) as i:
                group(i, True, False)
            group(GROUPS - 1, False, False)

            with act.Fori(0, 2) as c:
                with act.Fori(0, 128 // UNROLL) as i:
                    for k in range(UNROLL):
                        t = c * 128 + i * UNROLL + k
                        w = bass.ds((i * UNROLL + k) * B, B)
                        now = k % 2
                        act.wait_ge(r_pre, t + 1)
                        act.activation(st["tr"][:, now, :], bank[0][:, w], ACT.Tanh, scale=0.5).then_inc(tr_ok, 1)
                        act.wait_ge(z_pre, t + 1)
                        act.activation(st["tz"][:, now, :], bank[1][:, w], ACT.Tanh, scale=0.5).then_inc(tz_ok, 1)
                        act.wait_ge(c_pre, t + 1)
                        act.activation(st["hh"][:, now, :], bank[2][:, w], ACT.Tanh).then_inc(hh_ok, 1)

            def tile(i, first):
                act.wait_ge(hist_ok, i * STEPS_TILE + STEPS_TILE + 2)
                if not first:
                    act.wait_ge(y_done, i)
                act.activation(hs[:, :, :], hist[:, bass.ds(i * STEPS_TILE, STEPS_TILE), :].rearrange("p t b -> p b t"),
                               ACT.Copy, scale=0.5)
                cp(xs[:, :, :], x1T[:, bass.ds(i * STEPS_TILE, STEPS_TILE), :].rearrange("p t b -> p b t")).then_inc(hs_ok, 1)
                act.wait_ge(fdve, i * FD + 2)
                act.activation(rw[:, :], top[:, 0:1], ACT.Tanh, scale=0.5).then_inc(rwt_ok, 1)
                act.wait_ge(fdve, i * FD + 7)
                act.activation(th[:, :, :], gm[:, :, :], ACT.Tanh, scale=0.5).then_inc(th_ok, 1)
                act.wait_ge(at_done, i + 1)
                cp(aT[:, :, :].rearrange("p a n -> p (a n)"), bank[7][:, :]).then_inc(aT_ok, 1)

            tile(0, True)
            with act.Fori(1, B * T // TOK) as i:
                tile(i, False)

        @block.vector
        def _(dve):
            cp = dve.tensor_copy
            count = [0]

            def link(ins):
                count[0] += 1
                ins.then_inc(dve_self, 1)
                dve.wait_ge(dve_self, count[0])

            dve.wait_ge(setup_pe, 1)
            cp(xT[:, 0:512], bank[0][:, :]).then_inc(setup_dve, 1)
            dve.wait_ge(setup_pe, 3)
            cp(xT[:, 512:1024], bank[1][:, :])
            dve.wait_ge(setup_act, 1)
            cp(condT[:, :], bank[2][:, 128:128 + B]).then_inc(setup_dve, 1)
            dve.wait_ge(setup_dve, 2)
            dve.tensor_scalar(ybias[:, :], condT[:, :], cols[:, 0:1], None, ALU.add).then_inc(setup_dve, 1)
            dve.wait_ge(setup_pe, 6)
            dve.wait_ge(setup_act, 1)
            for b in range(B):
                ins = dve.scalar_tensor_tensor(mix[:, b, :], bank[5][:, b * 128:(b + 1) * 128], 1.0 / (D * RANK), wT[:, :],
                                               ALU.mult, ALU.add)
            ins.then_inc(setup_dve, 2)
            dve.wait_ge(consts, 5)
            dve.tensor_scalar(rext[:, 0:T - POS], rext[:, 0:T - POS], rel_end[:, 0:1], None, ALU.add).then_inc(setup_dve, 1)
            dve.tensor_scalar(rext[:, T + POS:RW], rext[:, T + POS:RW], rel_end[:, 1:2], None, ALU.add).then_inc(setup_dve, 1)
            dve.wait_ge(setup_pe, 14)
            cp(gateT[:, :], bank[3][:, 0:EXPERTS]).then_inc(setup_dve, 1)
            for k in range(3):
                dve.tensor_scalar(vbias[:, k, :], bank[3][:, 16 + 4 * k:20 + 4 * k], cols[:, 2 + k:3 + k], None,
                                  ALU.add).then_inc(setup_dve, 1)

            for n, item in enumerate(KQV):
                if n % 2 == 1:
                    dve.wait_ge(kqv_pe, n + 1)
                    kqv_out(item, bank[n % 8], cp).then_inc(kqv_dve, 1)

            for k in range(3):
                link(cp(parts[:, k, 0, :], wu[:, k, :]))
                link(dve.tensor_tensor(up32[:, :], wu[:, k, :], parts[:, k, 0, :], ALU.subtract))
                link(cp(parts[:, k, 1, :], up32[:, :]))
                link(dve.tensor_tensor(parts[:, k, 2, :], up32[:, :], parts[:, k, 1, :], ALU.subtract))
                for use, s in enumerate((0.5, -0.25) if k < 2 else (0.25,)):
                    for low in range(2):
                        ins = dve.tensor_scalar(uw[:, k, use, low, :, :], parts[:, k, :, :], s / SPLIT ** low, None, ALU.mult)
            ins.then_inc(gru_init, 1)

            def scores(g, u, first):
                n = g * PAIRS + u
                dve.wait_ge(qk_done, n + 1)
                dve.wait_ge(pos_in[u], 32 * g + 32)
                if not (first and u < 2):
                    dve.wait_ge(p_ready, n - 1)
                dve.memset(pad[:, u % 2:u % 2 + 1], 0.0)
                dve.tensor_tensor_reduce(out=s_sb[:, u % 2, :], in0=bank[2 + u % 2][:, 0:T], in1=pos[:, u, :], scale=-SCALE,
                                         scalar=LOWEST, op0=ALU.add, op1=ALU.min, accum_out=nmax[:, u:u + 1]).then_inc(s_ready, 1)

            def move_pt(g, u, first):
                n = g * PAIRS + u
                dve.wait_ge(t_done, n + 1)
                if not (first and u < 2):
                    dve.wait_ge(pv_done, n - 1)
                cp(pt_sb[:, u % 2, :], bank[4 + u % 2][:, 0:T]).then_inc(pt_ready, 1)
                dve.reciprocal(rinv[:, u:u + 1], rsum[:, u:u + 1]).then_inc(rinv_ready, 1)

            def normalize(g, u, first):
                n = g * PAIRS + u
                dve.wait_ge(pv_done, n + 1)
                dve.wait_ge(rinv_ready, n + 1)
                if u == 0 and not first:
                    dve.wait_ge(ot_done, g)
                for e in range(2):
                    h = slice(e * CH, (e + 1) * CH)
                    ins = dve.tensor_scalar(o_sb[h, u, :], bank[4 + u % 2][h, T + e * DH:T + (e + 1) * DH], rinv[h, u:u + 1],
                                            None, ALU.mult)
                ins.then_inc(o_ready, 1)

            def group(g, first):
                for u in range(PAIRS + 2):
                    if u < PAIRS:
                        scores(g, u, first)
                    if 1 <= u <= PAIRS:
                        move_pt(g, u - 1, first)
                    if u >= 2:
                        normalize(g, u - 2, first)
                dve.wait_ge(wo_done, g + 1)
                dve.scalar_tensor_tensor(x1f[:, bass.DynSlice((g // B) * CH * B + g % B, CH, B)], bank[7][:, 0:CH], cols[:, 1:2],
                                         xT[:, bass.ds((g % B) * T + (g // B) * CH, CH)], ALU.add, ALU.add).then_inc(x1_ready, 1)

            x1f = x1T[:, :, :].rearrange("p t b -> p (t b)")
            group(0, True)
            with dve.Fori(1, GROUPS) as i:
                group(i, False)

            for n in ("d", "d8"):
                dve.memset(st[n][:, 1, :], 0.0).then_inc(gru_init, 1)
            for n, s in (("b1", b1_ok), ("b2", b2_ok), ("g1", g1_ok), ("g2", g2_ok)):
                dve.memset(st[n][:, 1, :], 0.0).then_inc(s, 1)
            dve.memset(st["b8"][:, 1, :], 0.0).then_inc(gru_init, 3)
            dve.wait_ge(gru_init, 6)
            dve.memset(st["z8"][:, 1, :], 0.0).then_inc(d_ok, 1)

            with dve.Fori(0, T // UNROLL) as i:
                for k in range(UNROLL):
                    t = i * UNROLL + k
                    now, before = k % 2, 1 - k % 2
                    s = {n: a[:, now, :] for n, a in st.items()}
                    prev = {n: a[:, before, :] for n, a in st.items()}
                    stt = dve.scalar_tensor_tensor
                    dve.wait_ge(d_ok, t + 1)
                    dve.wait_ge(tr_ok, t + 1)
                    stt(s["q1"], s["tr"], 1.0, prev["d"], ALU.add, ALU.mult).then_inc(q1_ok, 1)
                    stt(s["q8"], s["tr"], 1.0, prev["d8"], ALU.add, ALU.mult).then_inc(q8_ok, 1)
                    dve.wait_ge(q8_ok, t + 1)
                    stt(s["q2"], s["q1"], -SPLIT, s["q8"], ALU.mult, ALU.add).then_inc(q2_ok, 1)
                    dve.wait_ge(tz_ok, t + 1)
                    stt(s["b1"], s["tz"], -1.0, prev["d"], ALU.add, ALU.mult).then_inc(b1_ok, 1)
                    stt(s["b8"], s["tz"], -1.0, prev["d8"], ALU.add, ALU.mult).then_inc(b8_ok, 1)
                    dve.tensor_scalar(s["z8"], s["tz"], 1.0, SPLIT, ALU.add, ALU.mult).then_inc(z8_ok, 1)
                    dve.wait_ge(b8_ok, t + 1)
                    stt(s["b2"], s["b1"], -SPLIT, s["b8"], ALU.mult, ALU.add).then_inc(b2_ok, 1)
                    dve.wait_ge(hh_ok, t + 1)
                    dve.wait_ge(z8_ok, t + 1)
                    stt(s["g1"], s["tz"], 1.0, s["hh"], ALU.add, ALU.mult).then_inc(g1_ok, 1)
                    dve.tensor_tensor(s["g8"], s["z8"], s["hh"], ALU.mult).then_inc(g8_ok, 1)
                    dve.wait_ge(g8_ok, t + 1)
                    stt(s["g2"], s["g1"], -SPLIT, s["g8"], ALU.mult, ALU.add).then_inc(g2_ok, 1)
                    stt(s["d8"], s["b8"], -0.5, s["g8"], ALU.mult, ALU.add).then_inc(d8_ok, 1)
                    dve.wait_ge(d8_ok, t + 1)
                    dve.wait_ge(hist_ok, t + 1)
                    dve.tensor_scalar(s["d"], s["d8"], 1.0 / SPLIT, None, ALU.mult).then_inc(d_ok, 1)

            def tile(i, first):
                n = [0]

                def step(ins, wait=True):
                    n[0] += 1
                    ins.then_inc(fdve, 1)
                    if wait:
                        dve.wait_ge(fdve, i * FD + n[0])

                dve.wait_ge(lg_done, i + 1)
                step(cp(lg[:, :], bank[3][:, 0:EXPERTS]))
                dve.memset(pad[:, 2:3], 0.0)
                step(dve.max(top[:, :], lg[:, :]))
                dve.memset(pad[:, 3:4], 0.0)
                step(dve.max_index(idx[:, :], top[:, :], lg[:, :]))
                step(cp(idxf[:, :], idx[:, 0:1]))
                dve.wait_ge(rwt_ok, i + 1)
                step(dve.tensor_scalar(rw2[:, :], rw[:, :], 0.5, 0.5, ALU.mult, ALU.add))
                step(dve.tensor_scalar(mask[:, :], iota[:, :], idxf[:, :], rw2[:, :], ALU.is_equal, ALU.mult))
                dve.wait_ge(gu_done, 2 * i + 2)
                m3 = mask[:, :].unsqueeze(2).broadcast_to([128, EXPERTS, HID])
                pre = lambda k: bank[k][:, :].rearrange("p (e n) -> p e n", e=EXPERTS)
                step(dve.tensor_tensor(gm[:, :, :], pre(4), m3, ALU.mult))
                step(dve.tensor_tensor(um[:, :, :], pre(5), m3, ALU.mult))
                dve.wait_ge(th_ok, i + 1)
                step(dve.scalar_tensor_tensor(sg[:, :, :], th[:, :, :], 1.0, gm[:, :, :], ALU.add, ALU.mult))
                step(dve.scalar_tensor_tensor(act_h[:, :, :], sg[:, :, :], 0.5, um[:, :, :], ALU.mult, ALU.mult))
                assert n[0] == FD - 1
                dve.wait_ge(y_done, i + 1)
                if not first:
                    dve.wait_ge(stored, i * 16 * B)
                ins = cp(y_out[:, :], bank[6][:, 0:D])
                step(ins)
                dve.wait_ge(fdve, i * FD + FD)
                dve.memset(idxf[:, :], 0.0).then_inc(y_ok, 1)

            tile(0, True)
            with dve.Fori(1, B * T // TOK) as i:
                tile(i, False)


KQV = [("q", a, s) for a in range(PAIRS) for s in range(2)] + [("k", a, s) for a in range(PAIRS) for s in range(2)] \
    + [("v", a, s) for a in range(B * T // 128) for s in range(2)]
KQV_ACT = (len(KQV) + 1) // 2
KQV_DVE = len(KQV) // 2
SETUP_ACT = 10
SETUP_DVE = 11
FD = 11


_INS = ['x', 'fside_Bx1x1024x16_0', 'cond_1024', 'L0_cond_W', 'L0_cond_fc_bias', 'L0_attn_Wq', 'L0_attn_Wkv', 'L0_attn_Wo',
        'L0_attn_bo', 'L0_attn_rel_emb', 'L0_cond2_W_z', 'L0_cond2_U_z', 'L0_cond2_C_z', 'L0_cond2_b_z', 'L0_cond2_W_r',
        'L0_cond2_U_r', 'L0_cond2_C_r', 'L0_cond2_b_r', 'L0_cond2_W', 'L0_cond2_U', 'L0_cond2_C', 'L0_cond2_b',
        'L0_ffn_gate_w', 'L0_ffn_w_gate', 'L0_ffn_w_up', 'L0_ffn_w_down']


def kernel(**inputs):
    import numpy as _np
    import concourse.bacc as _bacc
    from concourse import mybir as _mybir
    from concourse.bass_utils import run_bass_kernel_spmd as _run

    nc = _bacc.Bacc("TRN2", target_bir_lowering=False, num_devices=1)
    arrays, args = {}, []
    for name in _INS:
        a = _np.ascontiguousarray(inputs[name])
        arrays[f"in_{name}"] = a
        args.append(nc.dram_tensor(f"in_{name}", a.shape, _mybir.dt.from_np(a.dtype), kind="ExternalInput").ap())
    out = nc.dram_tensor("out", (B, T, D), _mybir.dt.float32, kind="ExternalOutput").ap()
    build(nc, *args, out)
    r = _run(nc, [arrays], core_ids=[0])
    return r.results[0]["out"]
```

```python
from contextlib import ExitStack

import concourse.bass as bass
from concourse import mybir

F32 = mybir.dt.float32
F16 = mybir.dt.float16
BF16 = mybir.dt.bfloat16
U32 = mybir.dt.uint32
ALU = mybir.AluOpType
ACT = mybir.ActivationFunctionType
AX_X = mybir.AxisListType.X

B, T, D = 4, 256, 128
RANK = 16
HEADS, DH = 16, 64
PAIRS = HEADS // 2
INNER = HEADS * DH
POS = 64
CH = 64
NCH = T // CH
GROUPS = NCH * B
RW = 2 * T - 1
EW = T + CH - 1
SCALE = DH ** -0.5
EXPERTS, HID = 8, 64
LOWEST = 3.0e38
SPLIT = 4096.0
PERIOD = 16
BLOCK = PERIOD // 2
EARLY = 5
OVERLAP = GROUPS - EARLY
WIDE = 48
TOK = 128
STEPS_TILE = TOK // B


def build(nc, x, side, cond, w_cond, fc_bias, wq, wkv, wo, bo, rel,
          w_z, u_z, c_z, b_z, w_r, u_r, c_r, b_r, w_c, u_c, c_c, b_c,
          gate_w, w_gate, w_up, w_down, out):
    with ExitStack() as ctx:
        def sb(name, shape, dt=F32):
            return ctx.enter_context(nc.sbuf_tensor(name, shape, dt))

        def sem(name):
            return ctx.enter_context(nc.semaphore(name))

        bank = [ctx.enter_context(nc.psum_tensor(f"bank{i}", [128, 512], F32)) for i in range(8)]
        skew = nc.dram_tensor("skew", (PAIRS, 128, EW), F32, kind="Internal").ap()

        ident = sb("ident", [128, 128])
        flip = sb("flip", [128, 128])
        ones4 = sb("ones4", [128, 4])
        x_nat = sb("x_nat", [128, B * T // 128, D])
        f_nat = sb("f_nat", [128, B, RANK])
        cond_nat = sb("cond_nat", [B, D])
        w_nat = sb("w_nat", [128, D])
        rel_nat = sb("rel_nat", [128, 2, DH])
        rel_end = sb("rel_end", [128, 2])
        cols = sb("cols", [128, 5])
        wq_sb = sb("wq_sb", [128, INNER])
        wkv_sb = sb("wkv_sb", [128, 2 * INNER])
        wo_sb = sb("wo_sb", [128, PAIRS, D])
        wx = sb("wx", [128, 3, D])
        wu = sb("wu", [128, 3, D])
        wc = sb("wc", [128, 3, D])
        gate_nat = sb("gate_nat", [EXPERTS, D])
        ffn_nat = sb("ffn_nat", [128, 3, 512])
        xT = sb("xT", [128, B * T])
        wT = sb("wT", [128, D])
        condT = sb("condT", [128, B])
        ybias = sb("ybias", [128, B])
        fT = sb("fT", [RANK, B, 128])
        mix = sb("mix", [128, B, D])
        yT = sb("yT", [128, B * T])
        kT = sb("kT", [128, B, PAIRS, T])
        qT = sb("qT", [128, NCH, B, PAIRS, CH])
        v_sb = sb("v_sb", [128, B, PAIRS, 2, 128])
        rext = sb("rext", [128, RW + 1])
        vbias = sb("vbias", [128, 3, B])
        ffnT = sb("ffnT", [128, 3, 512])
        gateT = sb("gateT", [128, EXPERTS])
        qa = sb("qa", [128, 2, 128])
        qb = sb("qb", [128, 2, 128])
        e_sb = sb("e_sb", [128, 4, EW])
        pos = sb("pos", [128, PAIRS, T])
        s_sb = sb("s_sb", [128, 2, T])
        p_sb = sb("p_sb", [128, 2, T])
        pt_sb = sb("pt_sb", [128, 2, T])
        nmax = sb("nmax", [128, PAIRS])
        rsum = sb("rsum", [128, PAIRS])
        rinv = sb("rinv", [128, PAIRS])
        o_sb = sb("o_sb", [128, PAIRS, DH])
        oT = sb("oT", [128, PAIRS, CH])
        x1T = sb("x1T", [128, T, B])
        up32 = sb("up32", [128, D])
        parts = sb("parts", [128, 3, 3, D], BF16)
        uw = sb("uw", [128, 3, 2, 3, D], BF16)
        trz = sb("trz", [128, 2, 2, B])
        st = {n: sb(n, [128, 2, WIDE if dt == F16 else B], dt) for n, dt in (
            ("hh", F32), ("d8", F32), ("q1", F16), ("q8", F32), ("q2", F16),
            ("b1", F16), ("b8", F32), ("b2", F16), ("z8", F32), ("g1", F16), ("g8", F32), ("g2", F16))}
        hist = x_nat[:, :, :].rearrange("p a d -> p (a d)").rearrange("p (t b) -> p t b", b=B)
        hs = sb("hs", [128, B, STEPS_TILE])
        xs = sb("xs", [128, B, STEPS_TILE])
        lg = sb("lg", [128, EXPERTS])
        top = sb("top", [128, 8])
        idx = sb("idx", [128, 8], U32)
        idxf = sb("idxf", [128, 1])
        rw = sb("rw", [128, 1])
        rw2 = sb("rw2", [128, 1])
        pad = sb("pad", [128, 4])
        hist_pad = sb("hist_pad", [128, 1])
        iota = sb("iota", [128, EXPERTS])
        mask = sb("mask", [128, EXPERTS])
        gm = sb("gm", [128, EXPERTS, HID])
        um = sb("um", [128, EXPERTS, HID])
        th = sb("th", [128, EXPERTS, HID])
        sg, act_h = th, um
        aT = sb("aT", [128, 4, 128])
        y_out = sb("y_out", [128, D])

        ld = {n: sem(f"ld_{n}") for n in ("x", "cond", "rel", "w", "att", "gru", "ffn")}
        consts = sem("consts")
        setup_pe = sem("setup_pe")
        setup_act = sem("setup_act")
        setup_dve = sem("setup_dve")
        dve_self = sem("dve_self")
        kqv_pe, kqv_act, kqv_dve = sem("kqv_pe"), sem("kqv_act"), sem("kqv_dve")
        qa_ready, qb_ready = sem("qa_ready"), sem("qb_ready")
        qr_done, e_ready = sem("qr_done"), sem("e_ready")
        e_stored = [sem(f"e_stored{u}") for u in range(PAIRS)]
        pos_in = [sem(f"pos_in{u}") for u in range(PAIRS)]
        qk_done, s_ready, p_ready = sem("qk_done"), sem("s_ready"), sem("p_ready")
        t_done, pt_ready, pv_done, o_ready = sem("t_done"), sem("pt_ready"), sem("pv_done"), sem("o_ready")
        rinv_ready = sem("rinv_ready")
        ot_done, oT_ready, wo_done, x1_ready = sem("ot_done"), sem("oT_ready"), sem("wo_done"), sem("x1_ready")
        u_self = sem("u_self")
        gru_init = sem("gru_init")
        bits_set, seed_ok = sem("bits_set"), sem("seed_ok")
        rz_pre, c_pre = sem("rz_pre"), sem("c_pre")
        trz_ok, hh_ok = sem("trz_ok"), sem("hh_ok")
        q1_ok, q8_ok, q2_ok = sem("q1_ok"), sem("q8_ok"), sem("q2_ok")
        b1_ok, b8_ok, b2_ok, z8_ok = sem("b1_ok"), sem("b8_ok"), sem("b2_ok"), sem("z8_ok")
        g1_ok, g8_ok, g2_ok, d8_ok = sem("g1_ok"), sem("g8_ok"), sem("g2_ok"), sem("d8_ok")
        hist_ok = sem("hist_ok")
        hs_ok, lg_done, gu_done, th_ok = sem("hs_ok"), sem("lg_done"), sem("gu_done"), sem("th_ok")
        rwt_ok, fdve, at_done, aT_ok, y_done, y_ok = (sem("rwt_ok"), sem("fdve"), sem("at_done"), sem("aT_ok"),
                                                      sem("y_done"), sem("y_ok"))
        act_free = sem("act_free")
        stored = sem("stored")

        block = ctx.enter_context(nc.Block())
        col = lambda v: v.rearrange("(p a) -> p a", a=1)

        def due(k, lag):
            for back in range(2):
                if (k + PERIOD * back - lag) % 2 == 0 and 0 <= k + PERIOD * back - lag < PERIOD:
                    return (k + PERIOD * back - lag) // 2, back
            return None

        def periods(engine, body):
            body(0, ((True, True), (False, False)), False)
            with engine.Fori(1, OVERLAP - 1) as i:
                body(i, ((True, True), (True, True)), False)
            body(OVERLAP - 1, ((True, False), (True, True)), False)
            body(OVERLAP, ((False, False), (True, False)), False)
            with engine.Fori(OVERLAP + 1, T // PERIOD - 1) as i:
                body(i, ((False, False), (False, False)), False)
            body(T // PERIOD - 1, ((False, False), (False, False)), True)

        def e_bank(u, beside):
            return bank[3] if beside else bank[u % 2]

        def s_bank(u, beside):
            return bank[4] if beside else bank[2 + u % 2]

        def o_bank(u, beside):
            return bank[6 + u % 2] if beside else bank[4 + u % 2]

        def rz_cols(k, gate=0, n=2 * B):
            at = (k % BLOCK * 2 + gate) * B
            return bank[k // BLOCK][:, at:at + n]

        def c_cols(k, n=B):
            return bank[2][:, k * B:k * B + n]

        def kqv_out(item, src, copy):
            kind, a, s = item
            if kind == "k":
                return copy(kT[:, 2 * s:2 * s + 2, a, :], src[:, :].rearrange("p (b n) -> p b n", b=2))
            if kind == "q":
                return copy(qT[:, :, 2 * s:2 * s + 2, a, :], src[:, :].rearrange("p (b c n) -> p c b n", b=2, c=NCH))
            return copy(v_sb[:, a // 2, 4 * s:4 * s + 4, a % 2, :], src[:, :].rearrange("p (h d) -> p h d", h=4))

        @block.sync
        def _(sp):
            sp.dma_start(x_nat[:, :, :], x.rearrange("b (a p) d -> p (b a) d", p=128)).then_inc(ld["x"], 16)
            sp.dma_start(f_nat[:, :, :], side.rearrange("b a p r -> p (b a) r")).then_inc(ld["cond"], 16)
            sp.dma_start(cond_nat[:, :], cond).then_inc(ld["cond"], 16)
            sp.dma_start(w_nat[:, :], w_cond).then_inc(ld["cond"], 16)
            for k, vec in enumerate((fc_bias, bo, b_r, b_z, b_c)):
                sp.dma_start(cols[:, k:k + 1], col(vec)).then_inc(ld["cond"], 16)
            for e in range(2):
                sp.dma_start(rel_nat[:, e, :], rel[0:128, :]).then_inc(ld["rel"], 16)
                sp.dma_start(rel_end[e * DH:(e + 1) * DH, 0:1], rel[2 * POS:2 * POS + 1, :].rearrange("a d -> d a")).then_inc(ld["rel"], 16)
                sp.dma_start(rel_end[e * DH:(e + 1) * DH, 1:2], rel[0:1, :].rearrange("a d -> d a")).then_inc(ld["rel"], 16)

            def skew_unit(g, u):
                sp.wait_ge(e_ready, g * PAIRS + u + 1)
                sp.dma_start(skew[u], e_sb[:, u % 4, :]).then_inc(e_stored[u], 16)

            def unskew_unit(g, u):
                sp.wait_ge(e_stored[u], g * 16 + 16)
                for e in range(2):
                    src = skew[u, e * CH:(e + 1) * CH, :].copy()
                    src = bass.AP(tensor=src.tensor, offset=src.offset + CH - 1, ap=[[EW - 1, CH], [1, T]])
                    sp.dma_start(pos[e * CH:(e + 1) * CH, u, :], src).then_inc(pos_in[u], 16)

            def skew_group(g):
                for u in range(PAIRS + 1):
                    if u < PAIRS:
                        skew_unit(g, u)
                    if u:
                        unskew_unit(g, u - 1)

            skew_group(0)
            with sp.Fori(0, GROUPS - 1) as i:
                skew_group(i + 1)

            with sp.Fori(0, B * T // TOK) as i:
                row = sp.snap(i * STEPS_TILE)
                sp.wait_ge(y_ok, i + 1)
                for b in range(B):
                    sp.dma_start(out[b, bass.ds(row, STEPS_TILE), :],
                                 y_out[b * STEPS_TILE:(b + 1) * STEPS_TILE, :]).then_inc(stored, 16)
            sp.wait_ge(stored, 16 * B * B * T // TOK)

        @block.gpsimd
        def _(pool):
            pool.memset(ident[:, :], 0.0).then_inc(consts, 1)
            pool.memset(flip[:, :], 0.0).then_inc(consts, 1)
            pool.memset(qa[:, :, :], 0.0).then_inc(consts, 1)
            pool.memset(qb[:, :, :], 0.0).then_inc(consts, 1)
            for e in range(EXPERTS):
                pool.memset(iota[:, e:e + 1], float(e))
            pool.memset(rext[:, :], 0.0).then_inc(consts, 1)
            pool.memset(hist_pad[:, :], 0.0).then_inc(hist_ok, 2)
            pool.wait_ge(consts, 5)
            pool.affine_select(out=ident[:, :], in_=ident[:, :], compare_op=ALU.not_equal, fill=1.0,
                               base=0, pattern=[[-1, 128]], channel_multiplier=1).then_inc(consts, 1)
            pool.affine_select(out=flip[:, :], in_=flip[:, :], compare_op=ALU.not_equal, fill=1.0,
                               base=-127, pattern=[[1, 128]], channel_multiplier=1).then_inc(consts, 1)

            def stage(dst, ready, used, g, u, first):
                n = g * PAIRS + u
                if not (first and u < 2):
                    pool.wait_ge(used, n - 1)
                for e in range(2):
                    h = slice(e * DH, (e + 1) * DH)
                    ins = pool.tensor_copy(dst[h, u % 2, e * CH:(e + 1) * CH], qT2[h, bass.ds(n * CH, CH)])
                ins.then_inc(ready, 1)

            qT2 = qT[:, :, :, :, :].rearrange("p c b h n -> p (c b h n)")
            pool.wait_ge(kqv_act, KQV_ACT)
            pool.wait_ge(kqv_dve, KQV_DVE)
            for u in range(PAIRS):
                stage(qa, qa_ready, qr_done, 0, u, True)

            def both(i, u):
                stage(qa, qa_ready, qr_done, i + 1, u, False)

            for u in range(PAIRS):
                both(0, u)
                stage(qb, qb_ready, qk_done, 0, u, True)
            with pool.Fori(1, EARLY) as i:
                for u in range(PAIRS):
                    both(i, u)
                    stage(qb, qb_ready, qk_done, i, u, False)
            stage(qb, qb_ready, qk_done, EARLY, 0, False)
            stage(qa, qa_ready, qr_done, EARLY + 1, 0, False)

            pool.wait_ge(qa_ready, (EARLY + 1) * PAIRS + 1)

            def period(i, qa_units, qb_units):
                for k in range(PERIOD):
                    if k % 2:
                        u, g = k // 2 + 1, i + EARLY
                        if u < qb_units:
                            pool.wait_ge(hist_ok, i * PERIOD + k + 2)
                            stage(qb, qb_ready, qk_done, g, u, False)
                        if u < qa_units:
                            stage(qa, qa_ready, qr_done, g + 1, u, False)
                            pool.wait_ge(qa_ready, (g + 1) * PAIRS + u + 1)
                        if u < qb_units:
                            pool.wait_ge(qb_ready, g * PAIRS + u + 1)
                    pool.wait_ge(d8_ok, i * PERIOD + k + 2)
                    pool.tensor_copy(hist[:, bass.ds(i * PERIOD + k, 1), :], st["d8"][:, k % 2:k % 2 + 1, :]).then_inc(hist_ok, 1)

            with pool.Fori(0, OVERLAP - 2) as i:
                period(i, PAIRS + 1, PAIRS + 1)
            period(OVERLAP - 2, PAIRS, PAIRS + 1)
            period(OVERLAP - 1, 0, PAIRS)
            with pool.Fori(OVERLAP, T // PERIOD) as i:
                period(i, 0, 0)

        @block.tensor
        def _(pe):
            mm = pe.matmul
            pe.wait_ge(consts, 7)
            pe.wait_ge(ld["x"], 16)
            for s in range(2):
                for k in range(4):
                    ins = pe.transpose(bank[s][:, k * 128:(k + 1) * 128], x_nat[:, s * 4 + k, :], ident[:, :])
                ins.then_inc(setup_pe, 1)
            pe.wait_ge(ld["cond"], 128)
            pe.transpose(bank[2][:, 0:128], w_nat[:, :], ident[:, :])
            pe.transpose(bank[2][:, 128:128 + B], cond_nat[:, :], ident[0:B, 0:B]).then_inc(setup_pe, 1)
            for b in range(B):
                ins = pe.transpose(bank[3][0:RANK, b * 128:(b + 1) * 128], f_nat[:, b, :], ident[:, :])
            ins.then_inc(setup_pe, 1)
            pe.wait_ge(ld["rel"], 96)
            pe.transpose(bank[4][:, 0:128], rel_nat[:, :, :].rearrange("p a d -> p (a d)"), flip[:, :]).then_inc(setup_pe, 1)
            pe.wait_ge(setup_act, 2)
            for b in range(B):
                ins = mm(bank[5][:, b * 128:(b + 1) * 128], fT[:, b, :], fT[:, b, :], start=True, stop=True)
            ins.then_inc(setup_pe, 1)
            pe.wait_ge(setup_dve, 5)
            pe.wait_ge(setup_act, 3)
            for b in range(B):
                mm(bank[7 - b][:, 0:T], mix[:, b, :], xT[:, b * T:(b + 1) * T],
                   start=True, stop=True).then_inc(setup_pe, 1)
            pe.wait_ge(ld["ffn"], 64)
            for j in range(3):
                for k in range(4):
                    ins = pe.transpose(bank[j][:, k * 128:(k + 1) * 128], ffn_nat[:, j, k * 128:(k + 1) * 128], ident[:, :])
                ins.then_inc(setup_pe, 1)
            pe.wait_ge(ld["gru"], 144)
            pe.transpose(bank[3][:, 0:EXPERTS], gate_nat[:, :], ident[0:EXPERTS, 0:EXPERTS])
            for k in range(3):
                ins = mm(bank[3][:, 16 + 4 * k:20 + 4 * k], wc[:, k, :], condT[:, :], start=True, stop=True)
            ins.then_inc(setup_pe, 1)

            pe.wait_ge(ld["att"], 48)
            pe.wait_ge(setup_act, 7)
            pe.wait_ge(setup_dve, SETUP_DVE)
            pe.wait_ge(setup_act, SETUP_ACT)
            for n, (kind, a, s) in enumerate(KQV):
                if n >= 8:
                    pe.wait_ge(*((kqv_act, n // 2 - 3) if n % 2 == 0 else (kqv_dve, (n - 1) // 2 - 3)))
                half = slice(s * 512, (s + 1) * 512)
                if kind == "k":
                    ins = mm(bank[n % 8][:, :], wkv_sb[:, a * 128:(a + 1) * 128], yT[:, half], start=True, stop=True)
                elif kind == "q":
                    ins = mm(bank[n % 8][:, :], wq_sb[:, a * 128:(a + 1) * 128], yT[:, half], start=True, stop=True)
                else:
                    ins = mm(bank[n % 8][:, :], yT[:, a * 128:(a + 1) * 128], wkv_sb[:, INNER + s * 512:INNER + (s + 1) * 512],
                             start=True, stop=True)
                ins.then_inc(kqv_pe, 1)

            kT2 = kT[:, :, :, :].rearrange("p b h n -> p (b h n)")
            v2 = v_sb[:, :, :, :, :].rearrange("p b h r d -> p (b h r d)")

            def positions(g, u, first, beside=False, half=None):
                n = g * PAIRS + u
                w, at = (EW, 0) if half is None else (EW - EW // 2, 0) if half == 0 else (EW // 2, EW - EW // 2)
                if half != 1:
                    pe.wait_ge(qa_ready, n + 1)
                    if beside:
                        pe.wait_ge(e_ready, n)
                    elif not (first and u < 2):
                        pe.wait_ge(e_ready, n - 1)
                ins = mm(e_bank(u, beside)[:, at:at + w], qa[:, u % 2, :], rext[:, bass.ds(T - CH - (g // B) * CH + at, w)],
                         start=True, stop=True)
                if half != 0:
                    ins.then_inc(qr_done, 1)

            def scores(g, u, first, beside=False):
                n = g * PAIRS + u
                pe.wait_ge(qb_ready, n + 1)
                if beside:
                    pe.wait_ge(s_ready, n)
                elif not (first and u < 2):
                    pe.wait_ge(s_ready, n - 1)
                mm(s_bank(u, beside)[:, 0:T], qb[:, u % 2, :], kT2[:, bass.ds(((g % B) * PAIRS + u) * T, T)],
                   start=True, stop=True).then_inc(qk_done, 1)

            def transpose_p(g, u, first, beside=False):
                n = g * PAIRS + u
                pe.wait_ge(p_ready, n + 1)
                if not (first and u < 2):
                    pe.wait_ge(o_ready, n - 1)
                for r in range(2):
                    ins = pe.transpose(o_bank(u, beside)[:, r * 128:(r + 1) * 128], p_sb[:, u % 2, r * 128:(r + 1) * 128], ident[:, :])
                ins.then_inc(t_done, 1)

            def values(g, u, beside=False):
                n = g * PAIRS + u
                pe.wait_ge(pt_ready, n + 1)
                for r in range(2):
                    ins = mm(o_bank(u, beside)[:, T:T + 128], pt_sb[:, u % 2, r * 128:(r + 1) * 128],
                             v2[:, bass.ds((((g % B) * PAIRS + u) * 2 + r) * 128, 128)], start=(r == 0), stop=(r == 1))
                ins.then_inc(pv_done, 1)

            def heads_apart(g, beside=False):
                pe.wait_ge(o_ready, g * PAIRS + PAIRS)
                for u in range(0, PAIRS, 2):
                    ins = pe.transpose(bank[5 if beside else 6][:, u * 64:u * 64 + 128],
                                       o_sb[:, u:u + 2, :].rearrange("p u d -> p (u d)"), ident[:, :])
                ins.then_inc(ot_done, 1)

            def project(g, units, beside=False):
                if units[0] == 0:
                    pe.wait_ge(oT_ready, g * 4 + 4)
                for u in units:
                    ins = mm(bank[5 if beside else 7][:, 0:CH], wo_sb[:, u, :], oT[:, u, :], start=(u == 0), stop=(u == PAIRS - 1))
                if units[-1] == PAIRS - 1:
                    ins.then_inc(wo_done, 1)

            def group(g, ahead, first):
                for u in range(PAIRS + 2):
                    if u < PAIRS:
                        if ahead:
                            positions(g + 1, u, False)
                        scores(g, u, first)
                    if 1 <= u <= PAIRS:
                        transpose_p(g, u - 1, first)
                    if u >= 2:
                        values(g, u - 2)
                if not first:
                    pe.wait_ge(x1_ready, g)
                heads_apart(g)
                project(g, range(PAIRS))

            pe.wait_ge(kqv_act, KQV_ACT)
            pe.wait_ge(kqv_dve, KQV_DVE)
            for u in range(PAIRS):
                positions(0, u, True)
            group(0, True, True)
            with pe.Fori(1, EARLY) as i:
                group(i, True, False)

            x1f = x1T[:, :, :].rearrange("p t b -> p (t b)")
            pe.wait_ge(x1_ready, EARLY)
            pe.wait_ge(e_ready, (EARLY + 1) * PAIRS)
            for k in range(3):
                ins = mm(bank[k][:, 0:128], ident[:, :], x1f[:, 0:128], start=True, stop=True)
            ins.then_inc(bits_set, 1)

            def inputs(i, block, gate):
                x_ = x1T[:, bass.ds(i * PERIOD + block * BLOCK, BLOCK), :]
                if gate < 2:
                    o_ = bank[block][:, 0:BLOCK * 2 * B].rearrange("p (t g b) -> p t g b", g=2, b=B)[:, :, gate, :]
                else:
                    o_ = bank[2][:, block * BLOCK * B:(block + 1) * BLOCK * B].rearrange("p (t b) -> p t b", b=B)
                mm(o_, wx[:, gate, :], x_, start=False, stop=True, skip_group_check=True)

            pe.wait_ge(seed_ok, 1)
            for gate in range(3):
                inputs(0, 0, gate)
            pe.wait_ge(gru_init, 5)

            def window(i, k, groups, last):
                g = i + EARLY
                for back, (there, ahead) in enumerate(groups):
                    if not there:
                        continue
                    if due(k, 2) and due(k, 2)[1] == back:
                        transpose_p(g - back, due(k, 2)[0], False, True)
                    if due(k, 3) and due(k, 3)[1] == back:
                        values(g - back, due(k, 3)[0], True)
                    if back == 0 and k % 2 == 0:
                        scores(g, k // 2, False, True)
                    if back == 0 and ahead:
                        positions(g + 1, k // 2, False, True, k % 2)
                    if back == 1 and k == 3:
                        pe.wait_ge(x1_ready, g - 1)
                        heads_apart(g - 1, True)
                    if back == 1 and 5 <= k < 9:
                        project(g - 1, (2 * k - 10, 2 * k - 9), True)
                if k in (3, 5, 7):
                    if k == 3:
                        pe.wait_ge(seed_ok, 2 * i + 2)
                    inputs(i, 1, k // 2 - 1)
                if k in (11, 13, 15) and not last:
                    if k == 11:
                        pe.wait_ge(seed_ok, 2 * i + 3)
                        pe.wait_ge(x1_ready, READY(i))
                    inputs(i + 1, 0, k // 2 - 5)

            def READY(i):
                return ((i + 1) // 4 + 1) * 4

            def period(i, groups, last):
                for k in range(PERIOD):
                    t = i * PERIOD + k
                    now, before = k % 2, 1 - k % 2
                    n = WIDE if groups[0][0] else B

                    def product(out_, gate, use, operand, low):
                        for j in range(3 - low):
                            ins = mm(out_, uw[:, gate, use, j, :], operand, start=False, stop=True, skip_group_check=True)
                        return ins

                    for use, name, ok in ((1, "b", (b1_ok, b2_ok)), (0, "g", (g1_ok, g2_ok))):
                        for low in range(2):
                            pe.wait_ge(ok[low], t + 1)
                            for gate in range(2):
                                ins = product(rz_cols(k, gate, n), gate, use, st[f"{name}{low + 1}"][:, before, 0:n], low)
                    ins.then_inc(rz_pre, 1)
                    window(i, k, groups, last)
                    pe.wait_ge(q1_ok, t + 1)
                    product(c_cols(k, n), 2, 0, st["q1"][:, now, 0:n], 0)
                    pe.wait_ge(q2_ok, t + 1)
                    product(c_cols(k, n), 2, 0, st["q2"][:, now, 0:n], 1).then_inc(c_pre, 1)

            periods(pe, period)

            pe.wait_ge(hh_ok, T)
            def tile(i, first):
                hflat = hs[:, :, :].rearrange("p b t -> p (b t)")
                pe.wait_ge(hs_ok, i + 1)
                if not first:
                    pe.wait_ge(fdve, i * FD)
                mm(bank[3][:, 0:EXPERTS], hflat, gateT[:, :], start=True, stop=True).then_inc(lg_done, 1)
                mm(bank[4][:, :], hflat, ffnT[:, 0, :], start=True, stop=True).then_inc(gu_done, 1)
                mm(bank[5][:, :], hflat, ffnT[:, 1, :], start=True, stop=True).then_inc(gu_done, 1)
                mm(bank[6][:, 0:D], xs[:, :, :].rearrange("p b t -> p (b t)"), ident[:, :], start=True, stop=False)
                pe.wait_ge(fdve, i * FD + FD - 1)
                for k in range(4):
                    ins = pe.transpose(bank[7][:, k * 128:(k + 1) * 128],
                                       act_h[:, 2 * k:2 * k + 2, :].rearrange("p e n -> p (e n)"), ident[:, :])
                ins.then_inc(at_done, 1)
                pe.wait_ge(aT_ok, i + 1)
                for k in range(4):
                    ins = mm(bank[6][:, 0:D], aT[:, k, :], ffnT[:, 2, k * 128:(k + 1) * 128], start=False, stop=(k == 3))
                ins.then_inc(y_done, 1)

            tile(0, True)
            with pe.Fori(1, B * T // TOK) as i:
                tile(i, False)

        @block.scalar
        def _(act):
            act.dma_start(wkv_sb[:, :], wkv).then_inc(ld["att"], 16)
            act.dma_start(wq_sb[:, :], wq).then_inc(ld["att"], 16)
            act.dma_start(wo_sb[:, :, :], wo.rearrange("(u p) d -> p u d", p=128)).then_inc(ld["att"], 16)
            for k, (w_, u_, c_) in enumerate(((w_r, u_r, c_r), (w_z, u_z, c_z), (w_c, u_c, c_c))):
                act.dma_start(wx[:, k, :], w_).then_inc(ld["gru"], 16)
                act.dma_start(wu[:, k, :], u_).then_inc(ld["gru"], 16)
                act.dma_start(wc[:, k, :], c_).then_inc(ld["gru"], 16)
            act.dma_start(gate_nat[:, :], gate_w).then_inc(ld["ffn"], 16)
            for j, w_ in enumerate((w_gate, w_up)):
                act.dma_start(ffn_nat[:, j, :].rearrange("p (a d) -> p a d", a=4),
                              w_.rearrange("e n d -> (e n) d").rearrange("(a p) d -> p a d", p=128)).then_inc(ld["ffn"], 16)
            act.dma_start(ffn_nat[:, 2, :].rearrange("p (e n) -> p e n", e=EXPERTS),
                          w_down.rearrange("e d n -> d e n")).then_inc(ld["ffn"], 16)
            cp = lambda o, i: act.activation(o, i, ACT.Copy)
            act.wait_ge(setup_pe, 3)
            cp(wT[:, :], bank[2][:, 0:128]).then_inc(setup_act, 1)
            act.wait_ge(setup_pe, 4)
            cp(fT[:, :, :].rearrange("p b n -> p (b n)"), bank[3][0:RANK, :]).then_inc(setup_act, 1)
            act.wait_ge(setup_pe, 5)
            cp(rext[:, T - POS:T + POS], bank[4][:, 0:128]).then_inc(setup_act, 1)
            act.wait_ge(setup_dve, 3)
            for b in range(B):
                act.wait_ge(setup_pe, 7 + b)
                act.activation(yT[:, b * T:(b + 1) * T], bank[7 - b][:, 0:T], ACT.Gelu,
                               bias=ybias[:, b:b + 1]).then_inc(setup_act, 1)
            for j in range(3):
                act.wait_ge(setup_pe, 11 + j)
                cp(ffnT[:, j, :], bank[j][:, :]).then_inc(setup_act, 1)

            for n, item in enumerate(KQV):
                if n % 2 == 0:
                    act.wait_ge(kqv_pe, n + 1)
                    kqv_out(item, bank[n % 8], cp).then_inc(kqv_act, 1)

            def move_e(g, u, first, beside=False):
                n = g * PAIRS + u
                act.wait_ge(qr_done, n + 1)
                if not (first and u < 4):
                    act.wait_ge(e_stored[(u - 4) % PAIRS], 16 * g + (16 if u >= 4 else 0))
                cp(e_sb[:, u % 4, :], e_bank(u, beside)[:, 0:EW]).then_inc(e_ready, 1)

            def exps(g, u, first):
                n = g * PAIRS + u
                act.wait_ge(s_ready, n + 1)
                if not (first and u < 2):
                    act.wait_ge(t_done, n - 1)
                act.activation(p_sb[:, u % 2, :], s_sb[:, u % 2, :], ACT.Exp, bias=nmax[:, u:u + 1], scale=-1.0,
                               accum_out=rsum[:, u:u + 1]).then_inc(p_ready, 1)

            def project(g, beside=False):
                act.wait_ge(ot_done, g + 1)
                for odd in range(2):
                    for e in range(2):
                        cp(oT[e * DH:(e + 1) * DH, odd::2, :],
                           bank[5 if beside else 6][odd * DH:(odd + 1) * DH, :].rearrange("p (u n) -> p u n", u=4)[:, :, e * CH:(e + 1) * CH]).then_inc(oT_ready, 1)

            def group(g, ahead, first):
                for u in range(PAIRS):
                    exps(g, u, first)
                    if ahead:
                        move_e(g + 1, u, False)
                project(g)

            for u in range(PAIRS):
                move_e(0, u, True)
            group(0, True, True)
            with act.Fori(1, EARLY) as i:
                group(i, True, False)

            def period(i, groups, last):
                g = i + EARLY
                for k in range(PERIOD):
                    for back, (there, ahead) in enumerate(groups):
                        if there and due(k, 2) and due(k, 2)[1] == back:
                            exps(g - back, due(k, 2)[0], False)
                            if ahead:
                                move_e(g - back + 1, due(k, 2)[0], False, True)
                        if there and back == 1 and k == 5:
                            project(g - 1, True)
                    t = i * PERIOD + k
                    now = k % 2
                    act.wait_ge(rz_pre, t + 1)
                    act.activation(trz[:, now, :, :].rearrange("p g b -> p (g b)"), rz_cols(k), ACT.Tanh, scale=0.5).then_inc(trz_ok, 1)
                    act.wait_ge(c_pre, t + 1)
                    act.activation(st["hh"][:, now, :], c_cols(k), ACT.Tanh).then_inc(hh_ok, 1)

            periods(act, period)

            def tile(i, first):
                act.wait_ge(hist_ok, i * STEPS_TILE + STEPS_TILE + 2)
                if not first:
                    act.wait_ge(y_done, i)
                act.activation(hs[:, :, :], hist[:, bass.ds(i * STEPS_TILE, STEPS_TILE), :].rearrange("p t b -> p b t"),
                               ACT.Copy, scale=0.5 / SPLIT)
                cp(xs[:, :, :], x1T[:, bass.ds(i * STEPS_TILE, STEPS_TILE), :].rearrange("p t b -> p b t")).then_inc(hs_ok, 1)
                act.wait_ge(fdve, i * FD + 2)
                act.activation(rw[:, :], top[:, 0:1], ACT.Tanh, scale=0.5).then_inc(rwt_ok, 1)
                act.wait_ge(fdve, i * FD + 7)
                act.activation(th[:, :, :], gm[:, :, :], ACT.Tanh, scale=0.5).then_inc(th_ok, 1)
                act.wait_ge(at_done, i + 1)
                cp(aT[:, :, :].rearrange("p a n -> p (a n)"), bank[7][:, :]).then_inc(aT_ok, 1)

            tile(0, True)
            with act.Fori(1, B * T // TOK) as i:
                tile(i, False)

        @block.vector
        def _(dve):
            cp = dve.tensor_copy
            count = [0]

            def link(ins):
                count[0] += 1
                ins.then_inc(dve_self, 1)
                dve.wait_ge(dve_self, count[0])

            dve.wait_ge(setup_pe, 1)
            cp(xT[:, 0:512], bank[0][:, :]).then_inc(setup_dve, 1)
            dve.wait_ge(setup_pe, 3)
            cp(xT[:, 512:1024], bank[1][:, :])
            dve.wait_ge(setup_act, 1)
            cp(condT[:, :], bank[2][:, 128:128 + B]).then_inc(setup_dve, 1)
            dve.wait_ge(setup_dve, 2)
            dve.tensor_scalar(ybias[:, :], condT[:, :], cols[:, 0:1], None, ALU.add).then_inc(setup_dve, 1)
            dve.wait_ge(setup_pe, 6)
            dve.wait_ge(setup_act, 1)
            for b in range(B):
                ins = dve.scalar_tensor_tensor(mix[:, b, :], bank[5][:, b * 128:(b + 1) * 128], 1.0 / (D * RANK), wT[:, :],
                                               ALU.mult, ALU.add)
            ins.then_inc(setup_dve, 2)
            dve.wait_ge(consts, 5)
            dve.tensor_scalar(rext[:, 0:T - POS], rext[:, 0:T - POS], rel_end[:, 0:1], None, ALU.add).then_inc(setup_dve, 1)
            dve.tensor_scalar(rext[:, T + POS:RW], rext[:, T + POS:RW], rel_end[:, 1:2], None, ALU.add).then_inc(setup_dve, 1)
            dve.wait_ge(setup_pe, 14)
            cp(gateT[:, :], bank[3][:, 0:EXPERTS]).then_inc(setup_dve, 1)
            for k in range(3):
                dve.tensor_scalar(vbias[:, k, :], bank[3][:, 16 + 4 * k:20 + 4 * k], cols[:, 2 + k:3 + k], None,
                                  ALU.add).then_inc(setup_dve, 1)

            for n, item in enumerate(KQV):
                if n % 2 == 1:
                    dve.wait_ge(kqv_pe, n + 1)
                    kqv_out(item, bank[n % 8], cp).then_inc(kqv_dve, 1)

            for k in range(3):
                link(cp(parts[:, k, 0, :], wu[:, k, :]))
                link(dve.tensor_tensor(up32[:, :], wu[:, k, :], parts[:, k, 0, :], ALU.subtract))
                link(cp(parts[:, k, 1, :], up32[:, :]))
                link(dve.tensor_tensor(parts[:, k, 2, :], up32[:, :], parts[:, k, 1, :], ALU.subtract))
                for use, s in enumerate((0.5, -0.25) if k < 2 else (0.25,)):
                    ins = dve.tensor_scalar(uw[:, k, use, :, :], parts[:, k, :, :], s / SPLIT, None, ALU.mult)
            ins.then_inc(gru_init, 1)

            def scores(g, u, first, beside=False):
                n = g * PAIRS + u
                dve.wait_ge(qk_done, n + 1)
                dve.wait_ge(pos_in[u], 32 * g + 32)
                if not (first and u < 2):
                    dve.wait_ge(p_ready, n - 1)
                dve.memset(pad[:, u % 2:u % 2 + 1], 0.0)
                dve.tensor_tensor_reduce(out=s_sb[:, u % 2, :], in0=s_bank(u, beside)[:, 0:T], in1=pos[:, u, :], scale=-SCALE,
                                         scalar=LOWEST, op0=ALU.add, op1=ALU.min, accum_out=nmax[:, u:u + 1]).then_inc(s_ready, 1)

            def move_pt(g, u, first, beside=False):
                n = g * PAIRS + u
                dve.wait_ge(t_done, n + 1)
                if not (first and u < 2):
                    dve.wait_ge(pv_done, n - 1)
                cp(pt_sb[:, u % 2, :], o_bank(u, beside)[:, 0:T]).then_inc(pt_ready, 1)
                dve.reciprocal(rinv[:, u:u + 1], rsum[:, u:u + 1]).then_inc(rinv_ready, 1)

            def normalize(g, u, first, beside=False):
                n = g * PAIRS + u
                dve.wait_ge(pv_done, n + 1)
                dve.wait_ge(rinv_ready, n + 1)
                if u == 0 and not first:
                    dve.wait_ge(ot_done, g)
                for e in range(2):
                    h = slice(e * CH, (e + 1) * CH)
                    ins = dve.tensor_scalar(o_sb[h, u, :], o_bank(u, beside)[h, T + e * DH:T + (e + 1) * DH], rinv[h, u:u + 1],
                                            None, ALU.mult)
                ins.then_inc(o_ready, 1)

            def residual(g, beside=False):
                dve.wait_ge(wo_done, g + 1)
                dve.scalar_tensor_tensor(x1f[:, bass.DynSlice((g // B) * CH * B + g % B, CH, B)], bank[5 if beside else 7][:, 0:CH],
                                         cols[:, 1:2], xT[:, bass.ds((g % B) * T + (g // B) * CH, CH)], ALU.add, ALU.add).then_inc(x1_ready, 1)

            def group(g, first):
                for u in range(PAIRS + 2):
                    if u < PAIRS:
                        scores(g, u, first)
                    if 1 <= u <= PAIRS:
                        move_pt(g, u - 1, first)
                    if u >= 2:
                        normalize(g, u - 2, first)
                residual(g)

            x1f = x1T[:, :, :].rearrange("p t b -> p (t b)")
            group(0, True)
            with dve.Fori(1, EARLY) as i:
                group(i, False)

            for n, ok in (("b1", b1_ok), ("b2", b2_ok), ("g1", g1_ok), ("g2", g2_ok), ("d8", d8_ok)):
                dve.memset(st[n][:, :, :], 0.0).then_inc(ok, 1)
            for n in ("q1", "q2"):
                dve.memset(st[n][:, :, :], 0.0)
            dve.memset(st["b8"][:, 1, :], 0.0).then_inc(gru_init, 4)

            def seed(block):
                cp(bank[block][:, 0:BLOCK * 2 * B].rearrange("p (t c) -> p t c", t=BLOCK),
                   vbias[:, 0:2, :].rearrange("p g b -> p (g b)").unsqueeze(1).broadcast_to([128, BLOCK, 2 * B]))
                cp(bank[2][:, block * BLOCK * B:(block + 1) * BLOCK * B].rearrange("p (t b) -> p t b", b=B),
                   vbias[:, 2:3, :].broadcast_to([128, BLOCK, B])).then_inc(seed_ok, 1)

            dve.wait_ge(gru_init, 5)
            dve.wait_ge(bits_set, 1)
            seed(0)

            def window(i, k, groups, last):
                g = i + EARLY
                for back, (there, ahead) in enumerate(groups):
                    if not there:
                        continue
                    if due(k, 4) and due(k, 4)[1] == back:
                        normalize(g - back, due(k, 4)[0], False, True)
                    if due(k, 2) and due(k, 2)[1] == back:
                        move_pt(g - back, due(k, 2)[0], False, True)
                    if back == 0 and k % 2:
                        scores(g, k // 2, False, True)
                    if back == 1 and k == 9:
                        residual(g - 1, True)
                if k == 1 or (k == 9 and not last):
                    seed(0 if k == 9 else 1)

            def period(i, groups, last):
                for k in range(PERIOD):
                    window(i, k, groups, last)
                    t = i * PERIOD + k
                    now, before = k % 2, 1 - k % 2
                    s = {n: a[:, now, 0:B] for n, a in st.items()}
                    tr, tz = trz[:, now, 0, :], trz[:, now, 1, :]
                    d8 = st["d8"][:, before, :]
                    stt = dve.scalar_tensor_tensor
                    dve.wait_ge(d8_ok, t + 1)
                    dve.wait_ge(trz_ok, t + 1)
                    stt(s["q1"], tr, 1.0, d8, ALU.add, ALU.mult).then_inc(q1_ok, 1)
                    stt(s["q8"], tr, 1.0, d8, ALU.add, ALU.mult).then_inc(q8_ok, 1)
                    stt(s["b1"], tz, -1.0, d8, ALU.add, ALU.mult).then_inc(b1_ok, 1)
                    dve.wait_ge(q8_ok, t + 1)
                    dve.tensor_tensor(s["q2"], s["q8"], s["q1"], ALU.subtract).then_inc(q2_ok, 1)
                    stt(s["b8"], tz, -1.0, d8, ALU.add, ALU.mult).then_inc(b8_ok, 1)
                    dve.tensor_scalar(s["z8"], tz, 1.0, SPLIT, ALU.add, ALU.mult).then_inc(z8_ok, 1)
                    dve.wait_ge(b8_ok, t + 1)
                    dve.tensor_tensor(s["b2"], s["b8"], s["b1"], ALU.subtract).then_inc(b2_ok, 1)
                    dve.wait_ge(z8_ok, t + 1)
                    dve.wait_ge(hh_ok, t + 1)
                    dve.tensor_tensor(s["g1"], s["z8"], s["hh"], ALU.mult).then_inc(g1_ok, 1)
                    dve.tensor_tensor(s["g8"], s["z8"], s["hh"], ALU.mult).then_inc(g8_ok, 1)
                    dve.wait_ge(g8_ok, t + 1)
                    dve.tensor_tensor(s["g2"], s["g8"], s["g1"], ALU.subtract).then_inc(g2_ok, 1)
                    dve.wait_ge(hist_ok, t + 1)
                    stt(s["d8"], s["b8"], -0.5, s["g8"], ALU.mult, ALU.add).then_inc(d8_ok, 1)

            periods(dve, period)

            def tile(i, first):
                n = [0]

                def step(ins, wait=True):
                    n[0] += 1
                    ins.then_inc(fdve, 1)
                    if wait:
                        dve.wait_ge(fdve, i * FD + n[0])

                dve.wait_ge(lg_done, i + 1)
                step(cp(lg[:, :], bank[3][:, 0:EXPERTS]))
                dve.memset(pad[:, 2:3], 0.0)
                step(dve.max(top[:, :], lg[:, :]))
                dve.memset(pad[:, 3:4], 0.0)
                step(dve.max_index(idx[:, :], top[:, :], lg[:, :]))
                step(cp(idxf[:, :], idx[:, 0:1]))
                dve.wait_ge(rwt_ok, i + 1)
                step(dve.tensor_scalar(rw2[:, :], rw[:, :], 0.5, 0.5, ALU.mult, ALU.add))
                step(dve.tensor_scalar(mask[:, :], iota[:, :], idxf[:, :], rw2[:, :], ALU.is_equal, ALU.mult))
                dve.wait_ge(gu_done, 2 * i + 2)
                m3 = mask[:, :].unsqueeze(2).broadcast_to([128, EXPERTS, HID])
                pre = lambda k: bank[k][:, :].rearrange("p (e n) -> p e n", e=EXPERTS)
                step(dve.tensor_tensor(gm[:, :, :], pre(4), m3, ALU.mult))
                step(dve.tensor_tensor(um[:, :, :], pre(5), m3, ALU.mult))
                dve.wait_ge(th_ok, i + 1)
                step(dve.scalar_tensor_tensor(sg[:, :, :], th[:, :, :], 1.0, gm[:, :, :], ALU.add, ALU.mult))
                step(dve.scalar_tensor_tensor(act_h[:, :, :], sg[:, :, :], 0.5, um[:, :, :], ALU.mult, ALU.mult))
                assert n[0] == FD - 1
                dve.wait_ge(y_done, i + 1)
                if not first:
                    dve.wait_ge(stored, i * 16 * B)
                ins = cp(y_out[:, :], bank[6][:, 0:D])
                step(ins)
                dve.wait_ge(fdve, i * FD + FD)
                dve.memset(idxf[:, :], 0.0).then_inc(y_ok, 1)

            tile(0, True)
            with dve.Fori(1, B * T // TOK) as i:
                tile(i, False)


KQV = [("q", a, s) for a in range(PAIRS) for s in range(2)] + [("k", a, s) for a in range(PAIRS) for s in range(2)] \
    + [("v", a, s) for a in range(B * T // 128) for s in range(2)]
KQV_ACT = (len(KQV) + 1) // 2
KQV_DVE = len(KQV) // 2
SETUP_ACT = 10
SETUP_DVE = 11
FD = 11


_INS = ['x', 'fside_Bx1x1024x16_0', 'cond_1024', 'L0_cond_W', 'L0_cond_fc_bias', 'L0_attn_Wq', 'L0_attn_Wkv', 'L0_attn_Wo',
        'L0_attn_bo', 'L0_attn_rel_emb', 'L0_cond2_W_z', 'L0_cond2_U_z', 'L0_cond2_C_z', 'L0_cond2_b_z', 'L0_cond2_W_r',
        'L0_cond2_U_r', 'L0_cond2_C_r', 'L0_cond2_b_r', 'L0_cond2_W', 'L0_cond2_U', 'L0_cond2_C', 'L0_cond2_b',
        'L0_ffn_gate_w', 'L0_ffn_w_gate', 'L0_ffn_w_up', 'L0_ffn_w_down']


def kernel(**inputs):
    import numpy as _np
    import concourse.bacc as _bacc
    from concourse import mybir as _mybir
    from concourse.bass_utils import run_bass_kernel_spmd as _run

    nc = _bacc.Bacc("TRN2", target_bir_lowering=False, num_devices=1)
    arrays, args = {}, []
    for name in _INS:
        a = _np.ascontiguousarray(inputs[name])
        arrays[f"in_{name}"] = a
        args.append(nc.dram_tensor(f"in_{name}", a.shape, _mybir.dt.from_np(a.dtype), kind="ExternalInput").ap())
    out = nc.dram_tensor("out", (B, T, D), _mybir.dt.float32, kind="ExternalOutput").ap()
    build(nc, *args, out)
    r = _run(nc, [arrays], core_ids=[0])
    return r.results[0]["out"]
```

```python
from contextlib import ExitStack

import concourse.bass as bass
from concourse import mybir

F32 = mybir.dt.float32
F16 = mybir.dt.float16
BF16 = mybir.dt.bfloat16
U32 = mybir.dt.uint32
ALU = mybir.AluOpType
ACT = mybir.ActivationFunctionType

B, T, D = 4, 256, 128
RANK = 16
HEADS, DH = 16, 64
PAIRS = HEADS // 2
INNER = HEADS * DH
POS = 64
CH = 64
NCH = T // CH
GROUPS = NCH * B
RW = 2 * T
EB = 2 * POS + 4
FILL = (RW - EB) // 2
EW = T + CH - 1
SCALE = DH ** -0.5
EXPERTS, HID = 8, 64
LOWEST = 3.0e38
SPLIT = 4096.0
PERIOD = 16
BLOCK = PERIOD // 2
EARLY = 5
OVERLAP = GROUPS - EARLY
WIDE_BESIDE, WIDE = 54, 60
FILLER = 512
TOK = 128
TILES = B * T // TOK
TILE_STEPS = 14
TILE_MAIN = (4, 5, 6, 7, 8, 11, 12)
STEPS_TILE = TOK // B


def build(nc, x, side, cond, w_cond, fc_bias, wq, wkv, wo, bo, rel,
          w_z, u_z, c_z, b_z, w_r, u_r, c_r, b_r, w_c, u_c, c_c, b_c,
          gate_w, w_gate, w_up, w_down, out):
    with ExitStack() as ctx:
        def sb(name, shape, dt=F32):
            return ctx.enter_context(nc.sbuf_tensor(name, shape, dt))

        def sem(name):
            return ctx.enter_context(nc.semaphore(name))

        bank = [ctx.enter_context(nc.psum_tensor(f"bank{i}", [128, 512], F32)) for i in range(8)]
        skew = nc.dram_tensor("skew", (PAIRS, 128, EW), F32, kind="Internal").ap()

        ident = sb("ident", [128, 128])
        flip = sb("flip", [128, 128])
        ones4 = sb("ones4", [128, 4])
        x_nat = sb("x_nat", [128, B * T // 128, D])
        f_nat = sb("f_nat", [128, B, RANK])
        cond_nat = sb("cond_nat", [B, D])
        w_nat = sb("w_nat", [128, D])
        rel_nat = sb("rel_nat", [128, 2, DH])
        rel_end = sb("rel_end", [128, 2])
        cols = sb("cols", [128, 5])
        wq_sb = sb("wq_sb", [128, INNER])
        wkv_sb = sb("wkv_sb", [128, 2 * INNER])
        wo_sb = sb("wo_sb", [128, PAIRS, D])
        wx = sb("wx", [128, 3, D])
        wu = sb("wu", [128, 3, D])
        wc = sb("wc", [128, 3, D])
        gate_nat = sb("gate_nat", [EXPERTS, D])
        ffn_nat = sb("ffn_nat", [128, 3, 512])
        xT = sb("xT", [128, B * T])
        wT = sb("wT", [128, D])
        condT = sb("condT", [128, B])
        ybias = sb("ybias", [128, B])
        fT = sb("fT", [RANK, B, 128])
        mix = sb("mix", [128, B, D])
        yT = sb("yT", [128, B * T])
        kT = sb("kT", [128, B, PAIRS, T])
        qT = sb("qT", [128, NCH, B, PAIRS, CH])
        v_sb = sb("v_sb", [128, B, PAIRS, 2, 128])
        rext = sb("rext", [128, EB])
        vbias = sb("vbias", [128, 3, B])
        ffnT = sb("ffnT", [128, 3, 512])
        gateT = sb("gateT", [128, EXPERTS])
        qa = sb("qa", [128, 2, 128])
        qb = sb("qb", [128, 2, 128])
        e_sb = sb("e_sb", [128, 4, RW])
        pos = sb("pos", [128, PAIRS, T])
        s_sb = sb("s_sb", [128, 2, T])
        p_sb = sb("p_sb", [128, 2, T])
        pt_sb = sb("pt_sb", [128, 2, T])
        nmax = sb("nmax", [128, PAIRS])
        rsum = sb("rsum", [128, PAIRS])
        rinv = sb("rinv", [128, PAIRS])
        o_sb = sb("o_sb", [128, PAIRS, DH])
        oT = sb("oT", [128, PAIRS, CH])
        x1T = sb("x1T", [128, T, B])
        up32 = sb("up32", [128, D])
        parts = sb("parts", [128, 2, 3, D], BF16)
        uw = sb("uw", [128, 2, 2, 3, D], BF16)
        uc = sb("uc", [128, D])
        trz = sb("trz", [128, 2, 2, B])
        st = {n: sb(n, [128, 2, WIDE if dt == F16 or n == "q8" else B], dt) for n, dt in (
            ("hh", F32), ("d8", F32), ("q8", F32),
            ("b1", F16), ("b8", F32), ("b2", F16), ("z8", F32), ("g1", F16), ("g8", F32), ("g2", F16))}
        hist = x_nat[:, :, :].rearrange("p a d -> p (a d)").rearrange("p (t b) -> p t b", b=B)
        hs = sb("hs", [128, B, STEPS_TILE])
        xs = sb("xs", [128, B, STEPS_TILE])
        lg = sb("lg", [128, EXPERTS])
        top = sb("top", [128, 8])
        idx = sb("idx", [128, 8], U32)
        idxf = sb("idxf", [128, 1])
        rw = sb("rw", [128, 1])
        rw2 = sb("rw2", [128, 1])
        act_pad = sb("act_pad", [128, 1])
        zeros = sb("zeros", [128, 512], F16)
        pad = sb("pad", [128, 4])
        hist_pad = sb("hist_pad", [128, 1])
        iota = sb("iota", [128, EXPERTS])
        mask = sb("mask", [128, EXPERTS])
        gm = sb("gm", [128, EXPERTS, HID])
        um = sb("um", [128, EXPERTS, HID])
        th = sb("th", [128, EXPERTS, HID])
        sg, act_h = th, um
        aT = sb("aT", [128, 4, 128])
        y_out = sb("y_out", [128, D])

        ld = {n: sem(f"ld_{n}") for n in ("x", "cond", "rel", "att", "gru", "ffn")}
        consts = sem("consts")
        zeros_ok = sem("zeros_ok")
        setup_pe = sem("setup_pe")
        setup_act = sem("setup_act")
        setup_dve = sem("setup_dve")
        kqv_pe, kqv_act, kqv_dve = sem("kqv_pe"), sem("kqv_act"), sem("kqv_dve")
        qa_ready, qb_ready = sem("qa_ready"), sem("qb_ready")
        qr_done, e_ready = sem("qr_done"), sem("e_ready")
        e_stored = [sem(f"e_stored{u}") for u in range(PAIRS)]
        pos_in = [sem(f"pos_in{u}") for u in range(PAIRS)]
        qk_done, s_ready, p_ready = sem("qk_done"), sem("s_ready"), sem("p_ready")
        t_done, pt_ready, pv_done, o_ready = sem("t_done"), sem("pt_ready"), sem("pv_done"), sem("o_ready")
        rinv_ready = sem("rinv_ready")
        ot_done, oT_ready, wo_done, x1_ready = sem("ot_done"), sem("oT_ready"), sem("wo_done"), sem("x1_ready")
        u_self = sem("u_self")
        gru_init = sem("gru_init")
        bits_set, seed_ok = sem("bits_set"), sem("seed_ok")
        rz_pre, c_pre = sem("rz_pre"), sem("c_pre")
        trz_ok, hh_ok = sem("trz_ok"), sem("hh_ok")
        q8_ok = sem("q8_ok")
        b1_ok, b8_ok, b2_ok, z8_ok = sem("b1_ok"), sem("b8_ok"), sem("b2_ok"), sem("z8_ok")
        g1_ok, g8_ok, g2_ok, d8_ok = sem("g1_ok"), sem("g8_ok"), sem("g2_ok"), sem("d8_ok")
        hist_ok = sem("hist_ok")
        hs_ok, xs_ok, th_ok, rwt_ok, aT_ok = sem("hs_ok"), sem("xs_ok"), sem("th_ok"), sem("rwt_ok"), sem("aT_ok")
        lg_done, g_done, u_done, at_done, y_done = sem("lg_done"), sem("g_done"), sem("u_done"), sem("at_done"), sem("y_done")
        lg_ok, top_ok, idx_ok, idxf_ok, mask_ok = sem("lg_ok"), sem("top_ok"), sem("idx_ok"), sem("idxf_ok"), sem("mask_ok")
        gm_ok, sg_ok, um_ok, ah_ok, y_ok = sem("gm_ok"), sem("sg_ok"), sem("um_ok"), sem("ah_ok"), sem("y_ok")
        stored = sem("stored")

        block = ctx.enter_context(nc.Block())
        col = lambda v: v.rearrange("(p a) -> p a", a=1)

        def due(k, lag):
            for back in range(2):
                if (k + PERIOD * back - lag) % 2 == 0 and 0 <= k + PERIOD * back - lag < PERIOD:
                    return (k + PERIOD * back - lag) // 2, back
            return None

        def periods(engine, body):
            none = ((False, False), (False, False))
            body(0, ((True, True), (False, False)), (), False)
            with engine.Fori(1, OVERLAP - 1) as i:
                body(i, ((True, True), (True, True)), (), False)
            body(OVERLAP - 1, ((True, False), (True, True)), (), False)
            body(OVERLAP, ((False, False), (True, False)), (), False)
            body(OVERLAP + 1, none, ((0, 0), (1, 0)), False)
            with engine.Fori(OVERLAP + 2, T // PERIOD - 1) as i:
                body(i, none, ((1, 1), (0, 0), (1, 0)), False)
            body(T // PERIOD - 1, none, ((1, 1), (0, 0)), True)

        def tiles_at(i, k, tiles):
            for j, back in tiles:
                step = k + PERIOD * back - BLOCK * j
                if 0 <= step < TILE_STEPS:
                    yield 2 * (i - back - OVERLAP - 1) + j, step

        def e_bank(u, beside):
            return bank[3] if beside else bank[u % 2]

        def s_bank(u, beside):
            return bank[4] if beside else bank[2 + u % 2]

        def o_bank(u, beside):
            return bank[6 + u % 2] if beside else bank[4 + u % 2]

        def rz_cols(k, gate=0, n=2 * B):
            at = (k % BLOCK * 2 + gate) * B
            return bank[k // BLOCK][:, at:at + n]

        def c_cols(k, n=B):
            return bank[2][:, k * B:k * B + n]

        def kqv_bank(n):
            return bank[2 + n % KQV_BANKS]

        def kqv_out(item, src, copy):
            kind, a, s = item
            if kind == "k":
                return copy(kT[:, 2 * s:2 * s + 2, a, :], src[:, :].rearrange("p (b n) -> p b n", b=2))
            if kind == "q":
                return copy(qT[:, :, 2 * s:2 * s + 2, a, :], src[:, :].rearrange("p (b c n) -> p c b n", b=2, c=NCH))
            return copy(v_sb[:, a // 2, 4 * s:4 * s + 4, a % 2, :], src[:, :].rearrange("p (h d) -> p h d", h=4))

        @block.sync
        def _(sp):
            sp.dma_start(x_nat[:, :, :], x.rearrange("b (a p) d -> p (b a) d", p=128)).then_inc(ld["x"], 16)
            sp.dma_start(f_nat[:, :, :], side.rearrange("b a p r -> p (b a) r")).then_inc(ld["cond"], 16)
            for e in range(2):
                sp.dma_start(rel_nat[:, e, :], rel[0:128, :]).then_inc(ld["rel"], 16)
                sp.dma_start(rel_end[e * DH:(e + 1) * DH, 0:1], rel[2 * POS:2 * POS + 1, :].rearrange("a d -> d a")).then_inc(ld["rel"], 16)
                sp.dma_start(rel_end[e * DH:(e + 1) * DH, 1:2], rel[0:1, :].rearrange("a d -> d a")).then_inc(ld["rel"], 16)
            sp.dma_start(wo_sb[:, :, :], wo.rearrange("(u p) d -> p u d", p=128)).then_inc(ld["att"], 16)
            for k, vec in enumerate((bo, b_r, b_z, b_c)):
                sp.dma_start(cols[:, k + 1:k + 2], col(vec)).then_inc(ld["gru"], 16)
            sp.dma_start(gate_nat[:, :], gate_w).then_inc(ld["ffn"], 16)
            for j, w_ in enumerate((w_gate, w_up)):
                sp.dma_start(ffn_nat[:, j, :].rearrange("p (a d) -> p a d", a=4),
                              w_.rearrange("e n d -> (e n) d").rearrange("(a p) d -> p a d", p=128)).then_inc(ld["ffn"], 16)
            sp.dma_start(ffn_nat[:, 2, :].rearrange("p (e n) -> p e n", e=EXPERTS),
                          w_down.rearrange("e d n -> d e n")).then_inc(ld["ffn"], 16)
            for k, (w_, u_, c_) in enumerate(((w_r, u_r, c_r), (w_z, u_z, c_z), (w_c, u_c, c_c))):
                sp.dma_start(wc[:, k, :], c_).then_inc(ld["gru"], 16)
                sp.dma_start(wx[:, k, :], w_).then_inc(ld["gru"], 16)
                sp.dma_start(wu[:, k, :], u_).then_inc(ld["gru"], 16)

            def skew_unit(g, u):
                sp.wait_ge(e_ready, g * PAIRS + u + 1)
                sp.dma_start(skew[u], e_sb[:, u % 4, bass.ds(T - CH - (g // B) * CH, EW)]).then_inc(e_stored[u], 16)

            def unskew_unit(g, u):
                sp.wait_ge(e_stored[u], g * 16 + 16)
                src = skew[u]
                src = bass.AP(tensor=src.tensor, offset=src.offset + CH - 1, ap=[[CH * EW, 2], [EW - 1, CH], [1, T]])
                sp.dma_start(pos[:, u, :], src).then_inc(pos_in[u], 16)

            def skew_group(g):
                for u in range(PAIRS + 1):
                    if u < PAIRS:
                        skew_unit(g, u)
                    if u:
                        unskew_unit(g, u - 1)

            skew_group(0)
            with sp.Fori(0, GROUPS - 1) as i:
                skew_group(i + 1)

            with sp.Fori(0, TILES) as i:
                row = sp.snap(i * STEPS_TILE)
                sp.wait_ge(y_ok, i + 1)
                sp.dma_start(out[:, bass.ds(row, STEPS_TILE), :], y_out[:, :]).then_inc(stored, 16)
            sp.wait_ge(stored, 16 * TILES)

        @block.gpsimd
        def _(pool):
            pool.memset(ident[:, :], 0.0).then_inc(consts, 1)
            pool.memset(flip[:, :], 0.0).then_inc(consts, 1)
            pool.memset(qa[:, :, :], 0.0).then_inc(consts, 1)
            pool.memset(qb[:, :, :], 0.0).then_inc(consts, 1)
            for e in range(EXPERTS):
                pool.memset(iota[:, e:e + 1], float(e))
            pool.memset(rext[:, :], 0.0).then_inc(consts, 1)
            pool.memset(zeros[:, :], 0.0).then_inc(zeros_ok, 1)
            pool.memset(hist_pad[:, :], 0.0).then_inc(hist_ok, 2)
            pool.wait_ge(consts, 5)
            pool.affine_select(out=ident[:, :], in_=ident[:, :], compare_op=ALU.not_equal, fill=1.0,
                               base=0, pattern=[[-1, 128]], channel_multiplier=1).then_inc(consts, 1)
            pool.affine_select(out=flip[:, :], in_=flip[:, :], compare_op=ALU.not_equal, fill=1.0,
                               base=-127, pattern=[[1, 128]], channel_multiplier=1).then_inc(consts, 1)

            def stage(dst, ready, used, g, u, first):
                n = g * PAIRS + u
                if not (first and u < 2):
                    pool.wait_ge(used, n - 1)
                for e in range(2):
                    h = slice(e * DH, (e + 1) * DH)
                    ins = pool.tensor_copy(dst[h, u % 2, e * CH:(e + 1) * CH], qT2[h, bass.ds(n * CH, CH)])
                ins.then_inc(ready, 1)

            qT2 = qT[:, :, :, :, :].rearrange("p c b h n -> p (c b h n)")
            pool.wait_ge(kqv_act, PAIRS)
            pool.wait_ge(kqv_dve, PAIRS)
            for u in range(PAIRS):
                stage(qa, qa_ready, qr_done, 0, u, True)

            def both(i, u):
                stage(qa, qa_ready, qr_done, i + 1, u, False)

            for u in range(PAIRS):
                both(0, u)
                stage(qb, qb_ready, qk_done, 0, u, True)
            with pool.Fori(1, EARLY) as i:
                for u in range(PAIRS):
                    both(i, u)
                    stage(qb, qb_ready, qk_done, i, u, False)
            pool.wait_ge(qb_ready, EARLY * PAIRS)

            def period(i, groups, tiles, last):
                g, (there, ahead) = i + EARLY, groups[0]
                for k in range(PERIOD):
                    if there and k % 2 == 0:
                        u = k // 2
                        pool.wait_ge(hist_ok, i * PERIOD + k + 2)
                        stage(qb, qb_ready, qk_done, g, u, False)
                        if ahead:
                            stage(qa, qa_ready, qr_done, g + 1, u, False)
                            pool.wait_ge(qa_ready, (g + 1) * PAIRS + u + 1)
                        pool.wait_ge(qb_ready, g * PAIRS + u + 1)
                    pool.wait_ge(d8_ok, i * PERIOD + k + 2)
                    pool.tensor_copy(hist[:, bass.ds(i * PERIOD + k, 1), :], st["d8"][:, k % 2:k % 2 + 1, :]).then_inc(hist_ok, 1)

            periods(pool, period)

        @block.tensor
        def _(pe):
            mm = pe.matmul
            pe.wait_ge(consts, 7)
            pe.wait_ge(ld["x"], 16)
            for s in range(2):
                for k in range(4):
                    ins = pe.transpose(bank[s][:, k * 128:(k + 1) * 128], x_nat[:, s * 4 + k, :], ident[:, :])
                ins.then_inc(setup_pe, 1)
            pe.wait_ge(ld["cond"], 64)
            pe.transpose(bank[2][:, 0:128], w_nat[:, :], ident[:, :])
            pe.transpose(bank[2][:, 128:128 + B], cond_nat[:, :], ident[0:B, 0:B]).then_inc(setup_pe, 1)
            for b in range(B):
                ins = pe.transpose(bank[3][0:RANK, b * 128:(b + 1) * 128], f_nat[:, b, :], ident[:, :])
            ins.then_inc(setup_pe, 1)
            pe.wait_ge(setup_act, 2)
            for b in range(B):
                ins = mm(bank[5][:, b * 128:(b + 1) * 128], fT[:, b, :], fT[:, b, :], start=True, stop=True)
            ins.then_inc(setup_pe, 1)
            pe.wait_ge(setup_dve, 5)
            for b in range(B):
                mm(bank[7 - b][:, 0:T], mix[:, b, :], xT[:, b * T:(b + 1) * T],
                   start=True, stop=True).then_inc(setup_pe, 1)
            pe.wait_ge(ld["rel"], 96)
            pe.transpose(bank[3][:, 0:128], rel_nat[:, :, :].rearrange("p a d -> p (a d)"), flip[:, :]).then_inc(setup_pe, 1)

            kT2 = kT[:, :, :, :].rearrange("p b h n -> p (b h n)")
            v2 = v_sb[:, :, :, :, :].rearrange("p b h r d -> p (b h r d)")

            def positions(g, u, first, beside=False):
                n = g * PAIRS + u
                pe.wait_ge(qa_ready, n + 1)
                if beside:
                    pe.wait_ge(e_ready, n)
                elif not (first and u < 2):
                    pe.wait_ge(e_ready, n - 1)
                mm(e_bank(u, beside)[:, 0:EB], qa[:, u % 2, :], rext[:, :], start=True, stop=True).then_inc(qr_done, 1)

            def scores(g, u, first, beside=False):
                n = g * PAIRS + u
                pe.wait_ge(qb_ready, n + 1)
                if beside:
                    pe.wait_ge(s_ready, n)
                elif not (first and u < 2):
                    pe.wait_ge(s_ready, n - 1)
                mm(s_bank(u, beside)[:, 0:T], qb[:, u % 2, :], kT2[:, bass.ds(((g % B) * PAIRS + u) * T, T)],
                   start=True, stop=True).then_inc(qk_done, 1)

            def transpose_p(g, u, first, beside=False):
                n = g * PAIRS + u
                pe.wait_ge(p_ready, n + 1)
                if not (first and u < 2):
                    pe.wait_ge(o_ready, n - 1)
                for r in range(2):
                    ins = pe.transpose(o_bank(u, beside)[:, r * 128:(r + 1) * 128], p_sb[:, u % 2, r * 128:(r + 1) * 128], ident[:, :])
                ins.then_inc(t_done, 1)

            def values(g, u, beside=False):
                n = g * PAIRS + u
                pe.wait_ge(pt_ready, n + 1)
                for r in range(2):
                    ins = mm(o_bank(u, beside)[:, T:T + 128], pt_sb[:, u % 2, r * 128:(r + 1) * 128],
                             v2[:, bass.ds((((g % B) * PAIRS + u) * 2 + r) * 128, 128)], start=(r == 0), stop=(r == 1))
                ins.then_inc(pv_done, 1)

            def heads_apart(g, beside=False, units=range(0, PAIRS, 2)):
                if units[0] == 0:
                    pe.wait_ge(o_ready, g * PAIRS + PAIRS)
                for u in units:
                    ins = pe.transpose(bank[5 if beside else 6][:, u * 64:u * 64 + 128],
                                       o_sb[:, u:u + 2, :].rearrange("p u d -> p (u d)"), ident[:, :])
                    if u % 4 == 2:
                        ins.then_inc(ot_done, 1)

            def project(g, units, beside=False):
                if units[0] == 0:
                    pe.wait_ge(oT_ready, g * 4 + 4)
                for u in units:
                    ins = mm(bank[5 if beside else 7][:, 0:CH], wo_sb[:, u, :], oT[:, u, :], start=(u == 0), stop=(u == PAIRS - 1))
                if units[-1] == PAIRS - 1:
                    ins.then_inc(wo_done, 1)

            pe.wait_ge(ld["att"], 48)
            pe.wait_ge(setup_dve, 7)
            pe.wait_ge(setup_act, 7)
            for n, (kind, a, s) in enumerate(KQV):
                if n >= KQV_BANKS:
                    pe.wait_ge(*((kqv_act, n // 2 - KQV_BANKS // 2 + 1) if n % 2 == 0 else (kqv_dve, n // 2 - KQV_BANKS // 2 + 1)))
                half = slice(s * 512, (s + 1) * 512)
                if kind == "k":
                    ins = mm(kqv_bank(n)[:, :], wkv_sb[:, a * 128:(a + 1) * 128], yT[:, half], start=True, stop=True)
                elif kind == "q":
                    ins = mm(kqv_bank(n)[:, :], wq_sb[:, a * 128:(a + 1) * 128], yT[:, half], start=True, stop=True)
                else:
                    ins = mm(kqv_bank(n)[:, :], yT[:, a * 128:(a + 1) * 128], wkv_sb[:, INNER + s * 512:INNER + (s + 1) * 512],
                             start=True, stop=True)
                ins.then_inc(kqv_pe, 1)
                if n in FIRST_E:
                    positions(0, FIRST_E.index(n), True)

            def unit_stages(g, u, first, before):
                if u == 2 and before:
                    pe.wait_ge(o_ready, g * PAIRS)
                    heads_apart(g - 1)
                positions(g + 1, u, False)
                scores(g, u, first)
                if u >= 1:
                    transpose_p(g, u - 1, first)
                elif before:
                    transpose_p(g - 1, PAIRS - 1, False)
                if u >= 2:
                    values(g, u - 2)
                elif before:
                    values(g - 1, PAIRS - 2 + u)
                if u == 3 and before:
                    project(g - 1, range(PAIRS))

            pe.wait_ge(kqv_act, KQV_ACT)
            pe.wait_ge(kqv_dve, KQV_DVE)
            pe.wait_ge(ld["ffn"], 64)
            for j in range(3):
                for k in range(4):
                    ins = pe.transpose(bank[2 + j][:, k * 128:(k + 1) * 128], ffn_nat[:, j, k * 128:(k + 1) * 128], ident[:, :])
                ins.then_inc(setup_pe, 1)
            pe.wait_ge(ld["gru"], 208)
            pe.transpose(bank[5][:, 0:EXPERTS], gate_nat[:, :], ident[0:EXPERTS, 0:EXPERTS])
            for k in range(3):
                ins = mm(bank[5][:, 16 + 4 * k:20 + 4 * k], wc[:, k, :], condT[:, :], start=True, stop=True)
            ins.then_inc(setup_pe, 1)
            pe.wait_ge(setup_act, SETUP_ACT)
            pe.wait_ge(setup_dve, SETUP_DVE)
            for u in range(PAIRS):
                unit_stages(0, u, True, False)
            for u in range(PAIRS):
                unit_stages(1, u, False, True)
            with pe.Fori(2, EARLY) as i:
                pe.wait_ge(x1_ready, i - 1)
                for u in range(PAIRS):
                    unit_stages(i, u, False, True)
            pe.wait_ge(x1_ready, EARLY - 1)
            transpose_p(EARLY - 1, PAIRS - 1, False)
            for u in (PAIRS - 2, PAIRS - 1):
                values(EARLY - 1, u)
            heads_apart(EARLY - 1)
            project(EARLY - 1, range(PAIRS))

            x1f = x1T[:, :, :].rearrange("p t b -> p (t b)")
            pe.wait_ge(x1_ready, EARLY)
            pe.wait_ge(e_ready, (EARLY + 1) * PAIRS)
            pe.wait_ge(zeros_ok, 1)
            for k in range(3):
                ins = mm(bank[k][:, :], uw[:, 0, 0, 0, :], zeros[:, :], start=True, stop=True)
            ins.then_inc(bits_set, 1)

            def inputs(i, block, gate):
                x_ = x1T[:, bass.ds(i * PERIOD + block * BLOCK, BLOCK), :]
                if gate < 2:
                    o_ = bank[block][:, 0:BLOCK * 2 * B].rearrange("p (t g b) -> p t g b", g=2, b=B)[:, :, gate, :]
                else:
                    o_ = bank[2][:, block * BLOCK * B:(block + 1) * BLOCK * B].rearrange("p (t b) -> p t b", b=B)
                mm(o_, wx[:, gate, :], x_, start=False, stop=True, skip_group_check=True)

            pe.wait_ge(seed_ok, 1)
            for gate in range(3):
                inputs(0, 0, gate)
            pe.wait_ge(gru_init, 5)

            def tile_product(tau, step, main):
                hflat = hs[:, :, :].rearrange("p b t -> p (b t)")
                n = 2 * step + main
                if n == 2:
                    pe.wait_ge(hs_ok, tau + 1)
                    mm(bank[3][:, 0:EXPERTS], hflat, gateT[:, :], start=True, stop=True).then_inc(lg_done, 1)
                if 9 <= n < 17:
                    j, q = divmod(n - 9, 4)
                    ins = mm(bank[4 + j][:, q * 128:(q + 1) * 128], hflat, ffnT[:, j, q * 128:(q + 1) * 128], start=True, stop=True)
                    if q == 3:
                        ins.then_inc((g_done, u_done)[j], 1)
                if n == 17:
                    pe.wait_ge(xs_ok, tau + 1)
                    mm(bank[6][:, 0:D], xs[:, :, :].rearrange("p b t -> p (b t)"), ident[:, :], start=True, stop=False)
                if n == 20:
                    pe.wait_ge(ah_ok, tau + 1)
                    for k in range(4):
                        ins = pe.transpose(bank[7][:, k * 128:(k + 1) * 128],
                                           act_h[:, 2 * k:2 * k + 2, :].rearrange("p e n -> p (e n)"), ident[:, :])
                    ins.then_inc(at_done, 1)
                if 22 <= n < 26:
                    q = n - 22
                    if q == 0:
                        pe.wait_ge(aT_ok, tau + 1)
                    ins = mm(bank[6][:, 0:D], aT[:, q, :], ffnT[:, 2, q * 128:(q + 1) * 128], start=False, stop=(q == 3))
                    if q == 3:
                        ins.then_inc(y_done, 1)

            WO = {8: (0, 1), 9: (2,), 10: (3, 4), 11: (5,), 12: (6, 7)}

            def first_window(i, k, groups, tiles, last):
                for back, (there, ahead) in enumerate(groups):
                    g = i + EARLY - back
                    if there and due(k, 4) and due(k, 4)[1] == back:
                        transpose_p(g, due(k, 4)[0], False, True)
                        if ahead:
                            positions(g + 1, due(k, 4)[0], False, True)
                    if there and due(k, 5) and due(k, 5)[1] == back:
                        values(g, due(k, 5)[0], True)
                if groups[1][0] and k == 5:
                    pe.wait_ge(x1_ready, i + EARLY - 1)
                    heads_apart(i + EARLY - 1, True, (0, 2))
                for tau, step in tiles_at(i, k, tiles):
                    tile_product(tau, step, 0)

            def main_window(i, k, groups, tiles, last):
                g = i + EARLY
                if groups[1][0] and k == 6:
                    heads_apart(g - 1, True, (4, 6))
                if groups[1][0] and k in WO:
                    project(g - 1, WO[k], True)
                if groups[0][0] and k % 2:
                    scores(g, k // 2, False, True)
                for tau, step in tiles_at(i, k, tiles):
                    tile_product(tau, step, 1)
                if not groups[0][0]:
                    free = bank[1 - k // BLOCK] if k not in (1, 9) else bank[3] if groups[1][0] else bank[7]
                    n = FILLER // 2 if any(s_ in TILE_MAIN for _, s_ in tiles_at(i, k, tiles)) else FILLER
                    mm(free[:, 0:n], uw[:, 0, 0, 0, :], zeros[:, 0:n], start=(k in (1, 9)), stop=True, skip_group_check=True)
                if k == 2:
                    pe.wait_ge(seed_ok, 2 * i + 2)
                    inputs(i, 1, 0)
                    inputs(i, 1, 1)
                if k == 4:
                    inputs(i, 1, 2)
                if k == 14 and not last:
                    pe.wait_ge(seed_ok, 2 * i + 3)
                    pe.wait_ge(x1_ready, READY(i))
                    inputs(i + 1, 0, 0)
                    inputs(i + 1, 0, 2)
                if k == 15 and not last:
                    inputs(i + 1, 0, 1)

            def READY(i):
                return ((i + 1) // 4 + 1) * 4

            def period(i, groups, tiles, last):
                for k in range(PERIOD):
                    t = i * PERIOD + k
                    now, before = k % 2, 1 - k % 2
                    n = WIDE_BESIDE if groups[0][0] else WIDE

                    def product(out_, gate, use, operand, low):
                        for j in range(3 - low):
                            ins = mm(out_, uw[:, gate, use, j, :], operand, start=False, stop=True, skip_group_check=True)
                        return ins

                    for use, name, ok in ((1, "b", (b1_ok, b2_ok)), (0, "g", (g1_ok, g2_ok))):
                        if name == "g":
                            first_window(i, k, groups, tiles, last)
                        for low in range(2):
                            pe.wait_ge(ok[low], t + 1)
                            for gate in range(2):
                                ins = product(rz_cols(k, gate, n), gate, use, st[f"{name}{low + 1}"][:, before, 0:n], low)
                    ins.then_inc(rz_pre, 1)
                    main_window(i, k, groups, tiles, last)
                    pe.wait_ge(q8_ok, t + 1)
                    mm(c_cols(k, n), uc[:, :], st["q8"][:, now, 0:n], start=False, stop=True, skip_group_check=True).then_inc(c_pre, 1)

            periods(pe, period)

            for step in range(TILE_STEPS):
                for main in range(2):
                    tile_product(TILES - 1, step, main)

        @block.scalar
        def _(act):
            act.dma_start(w_nat[:, :], w_cond).then_inc(ld["cond"], 16)
            act.dma_start(cond_nat[:, :], cond).then_inc(ld["cond"], 16)
            act.dma_start(cols[:, 0:1], col(fc_bias)).then_inc(ld["cond"], 16)
            act.dma_start(wq_sb[:, :], wq).then_inc(ld["att"], 16)
            act.dma_start(wkv_sb[:, :], wkv).then_inc(ld["att"], 16)
            cp = lambda o, i: act.activation(o, i, ACT.Copy)
            act.wait_ge(consts, 7)
            act.activation(act_pad[:, :], ident[:, 0:1], ACT.Gelu)
            act.wait_ge(setup_pe, 3)
            cp(wT[:, :], bank[2][:, 0:128]).then_inc(setup_act, 1)
            act.wait_ge(setup_pe, 4)
            cp(fT[:, :, :].rearrange("p b n -> p (b n)"), bank[3][0:RANK, :]).then_inc(setup_act, 1)
            act.wait_ge(setup_dve, 3)
            for b in range(B):
                act.wait_ge(setup_pe, 6 + b)
                act.activation(yT[:, b * T:(b + 1) * T], bank[7 - b][:, 0:T], ACT.Gelu,
                               bias=ybias[:, b:b + 1]).then_inc(setup_act, 1)
            act.wait_ge(setup_pe, 10)
            act.wait_ge(consts, 5)
            cp(rext[:, 2:EB - 2], bank[3][:, 0:128]).then_inc(setup_act, 1)


            def move_e(g, u, first, beside=False):
                n = g * PAIRS + u
                act.wait_ge(qr_done, n + 1)
                if not (first and u < 4):
                    act.wait_ge(e_stored[(u - 4) % PAIRS], 16 * g + (16 if u >= 4 else 0))
                cp(e_sb[:, u % 4, FILL:FILL + EB], e_bank(u, beside)[:, 0:EB])
                ends, row = e_bank(u, beside)[:, 0:2], e_sb[:, u % 4, 0:2]
                cp(bass.AP(tensor=row.tensor, offset=row.offset, ap=[row.ap[0], [FILL + EB, 2], [1, FILL]]),
                   bass.AP(tensor=ends.tensor, offset=ends.offset, ap=[ends.ap[0], [EB - 1, 2], [0, FILL]])).then_inc(e_ready, 1)

            def exps(g, u, first):
                n = g * PAIRS + u
                act.wait_ge(s_ready, n + 1)
                if not (first and u < 2):
                    act.wait_ge(t_done, n - 1)
                act.activation(p_sb[:, u % 2, :], s_sb[:, u % 2, :], ACT.Exp, bias=nmax[:, u:u + 1], scale=-1.0,
                               accum_out=rsum[:, u:u + 1]).then_inc(p_ready, 1)

            def move_pt(g, u):
                act.wait_ge(t_done, g * PAIRS + u + 1)
                cp(pt_sb[:, u % 2, :], o_bank(u, True)[:, 0:T]).then_inc(pt_ready, 1)

            def project(g, beside=False, turns=(0, 1)):
                if turns[0] == 0:
                    act.wait_ge(ot_done, 2 * g + 2)
                for odd in turns:
                    for e in range(2):
                        cp(oT[e * DH:(e + 1) * DH, odd::2, :],
                           bank[5 if beside else 6][odd * DH:(odd + 1) * DH, :].rearrange("p (u n) -> p u n", u=4)[:, :, e * CH:(e + 1) * CH]).then_inc(oT_ready, 1)

            for n, item in enumerate(KQV):
                if n % 2 == 0:
                    act.wait_ge(kqv_pe, n + 1)
                    kqv_out(item, kqv_bank(n), cp).then_inc(kqv_act, 1)
                if n in FIRST_E:
                    move_e(0, FIRST_E.index(n), True)

            for j in range(3):
                act.wait_ge(setup_pe, 11 + j)
                cp(ffnT[:, j, :], bank[2 + j][:, :]).then_inc(setup_act, 1)

            def unit_stages(g, u, first, before):
                exps(g, u, first)
                move_e(g + 1, u, False)
                if u == 2 and before:
                    project(g - 1)

            for u in range(PAIRS):
                unit_stages(0, u, True, False)
            with act.Fori(1, EARLY) as i:
                for u in range(PAIRS):
                    unit_stages(i, u, False, True)
            project(EARLY - 1)

            def tile_stage(tau, step, early):
                part = bass.ds(tau * STEPS_TILE, STEPS_TILE)
                if (step, early) == (0, False):
                    act.wait_ge(hist_ok, tau * STEPS_TILE + STEPS_TILE + 2)
                    act.activation(hs[:, :, :], hist[:, part, :].rearrange("p t b -> p b t"), ACT.Copy,
                                   scale=0.5 / SPLIT).then_inc(hs_ok, 1)
                if (step, early) == (1, True):
                    cp(xs[:, :, :], x1T[:, part, :].rearrange("p t b -> p b t")).then_inc(xs_ok, 1)
                if (step, early) == (3, True):
                    act.wait_ge(top_ok, tau + 1)
                    act.activation(rw[:, :], top[:, 0:1], ACT.Tanh, scale=0.5).then_inc(rwt_ok, 1)
                if (step, early) == (7, True):
                    act.wait_ge(gm_ok, tau + 1)
                    act.activation(th[:, :, :], gm[:, :, :], ACT.Tanh, scale=0.5).then_inc(th_ok, 1)
                if (step, early) == (10, False):
                    act.wait_ge(at_done, tau + 1)
                    cp(aT[:, :, :].rearrange("p a n -> p (a n)"), bank[7][:, :]).then_inc(aT_ok, 1)

            def period(i, groups, tiles, last):
                g = i + EARLY
                for k in range(PERIOD):
                    for back, (there, ahead) in enumerate(groups):
                        if there and due(k, 3) and due(k, 3)[1] == back:
                            exps(g - back, due(k, 3)[0], False)
                        if there and back == 1 and k == 8:
                            project(g - 1, True)
                    for tau, step in tiles_at(i, k, tiles):
                        tile_stage(tau, step, True)
                    t = i * PERIOD + k
                    now = k % 2
                    act.wait_ge(rz_pre, t + 1)
                    act.activation(trz[:, now, :, :].rearrange("p g b -> p (g b)"), rz_cols(k), ACT.Tanh, scale=0.5).then_inc(trz_ok, 1)
                    for back, (there, ahead) in enumerate(groups):
                        if there and ahead and due(k, 5) and due(k, 5)[1] == back:
                            move_e(g - back + 1, due(k, 5)[0], False, True)
                    for back in range(2):
                        if groups[back][0] and due(k, 4) and due(k, 4)[1] == back:
                            move_pt(g - back, due(k, 4)[0])
                    for tau, step in tiles_at(i, k, tiles):
                        tile_stage(tau, step, False)
                    act.wait_ge(c_pre, t + 1)
                    act.activation(st["hh"][:, now, :], c_cols(k), ACT.Tanh).then_inc(hh_ok, 1)

            periods(act, period)
            for step in range(TILE_STEPS):
                for early in (True, False):
                    tile_stage(TILES - 1, step, early)

        @block.vector
        def _(dve):
            cp = dve.tensor_copy
            dve.wait_ge(setup_pe, 1)
            cp(xT[:, 0:512], bank[0][:, :]).then_inc(setup_dve, 1)
            dve.wait_ge(setup_pe, 3)
            cp(xT[:, 512:1024], bank[1][:, :])
            dve.wait_ge(setup_act, 1)
            cp(condT[:, :], bank[2][:, 128:128 + B]).then_inc(setup_dve, 1)
            dve.wait_ge(setup_dve, 2)
            dve.tensor_scalar(ybias[:, :], condT[:, :], cols[:, 0:1], None, ALU.add).then_inc(setup_dve, 1)
            dve.wait_ge(setup_pe, 5)
            dve.wait_ge(setup_act, 1)
            for b in range(B):
                ins = dve.scalar_tensor_tensor(mix[:, b, :], bank[5][:, b * 128:(b + 1) * 128], 1.0 / (D * RANK), wT[:, :],
                                               ALU.mult, ALU.add)
            ins.then_inc(setup_dve, 2)
            dve.wait_ge(consts, 5)
            dve.wait_ge(ld["rel"], 96)
            dve.tensor_scalar(rext[:, 0:2], rext[:, 0:2], rel_end[:, 0:1], None, ALU.add).then_inc(setup_dve, 1)
            dve.tensor_scalar(rext[:, EB - 2:EB], rext[:, EB - 2:EB], rel_end[:, 1:2], None, ALU.add).then_inc(setup_dve, 1)
            def split_u(j):
                k, step = divmod(j, 6)
                if k == 2:
                    return dve.tensor_scalar(uc[:, :], wu[:, 2, :], 0.25 / SPLIT, None, ALU.mult)
                if j:
                    dve.wait_ge(u_self, j)
                if step == 0:
                    ins = cp(parts[:, k, 0, :], wu[:, k, :])
                elif step == 1:
                    ins = dve.tensor_tensor(up32[:, :], wu[:, k, :], parts[:, k, 0, :], ALU.subtract)
                elif step == 2:
                    ins = cp(parts[:, k, 1, :], up32[:, :])
                elif step == 3:
                    ins = dve.tensor_tensor(parts[:, k, 2, :], up32[:, :], parts[:, k, 1, :], ALU.subtract)
                else:
                    use, scale = ((0, 0.5), (1, -0.25))[step - 4]
                    ins = dve.tensor_scalar(uw[:, k, use, :, :], parts[:, k, :, :], scale / SPLIT, None, ALU.mult)
                ins.then_inc(u_self, 1)
                return ins

            dve.wait_ge(ld["gru"], 208)
            for n, item in enumerate(KQV):
                if n % 2 == 1 and n // 2 < 13:
                    split_u(n // 2)
                if n % 2 == 1:
                    dve.wait_ge(kqv_pe, n + 1)
                    kqv_out(item, kqv_bank(n), cp).then_inc(kqv_dve, 1)

            dve.wait_ge(setup_pe, 14)
            cp(gateT[:, :], bank[5][:, 0:EXPERTS]).then_inc(setup_dve, 1)
            for k in range(3):
                dve.tensor_scalar(vbias[:, k, :], bank[5][:, 16 + 4 * k:20 + 4 * k], cols[:, 2 + k:3 + k], None,
                                  ALU.add).then_inc(setup_dve, 1)


            for n, ok in (("b1", b1_ok), ("b2", b2_ok), ("g1", g1_ok), ("g2", g2_ok), ("d8", d8_ok)):
                dve.memset(st[n][:, :, :], 0.0).then_inc(ok, 1)
            dve.memset(st["q8"][:, :, :], 0.0)
            dve.memset(st["b8"][:, 1, :], 0.0).then_inc(gru_init, 5)

            def scores(g, u, first, beside=False):
                n = g * PAIRS + u
                dve.wait_ge(qk_done, n + 1)
                dve.wait_ge(pos_in[u], 16 * g + 16)
                if not (first and u < 2):
                    dve.wait_ge(p_ready, n - 1)
                dve.memset(pad[:, u % 2:u % 2 + 1], 0.0)
                dve.tensor_tensor_reduce(out=s_sb[:, u % 2, :], in0=s_bank(u, beside)[:, 0:T], in1=pos[:, u, :], scale=-SCALE,
                                         scalar=LOWEST, op0=ALU.add, op1=ALU.min, accum_out=nmax[:, u:u + 1]).then_inc(s_ready, 1)

            def invert(u):
                dve.reciprocal(rinv[:, u:u + 1], rsum[:, u:u + 1]).then_inc(rinv_ready, 1)

            def move_pt(g, u, first):
                n = g * PAIRS + u
                dve.wait_ge(t_done, n + 1)
                if not (first and u < 2):
                    dve.wait_ge(pv_done, n - 1)
                cp(pt_sb[:, u % 2, :], o_bank(u, False)[:, 0:T]).then_inc(pt_ready, 1)
                invert(u)

            def normalize(g, u, first, beside=False, heads=(0, 1)):
                n = g * PAIRS + u
                if heads[0] == 0:
                    dve.wait_ge(pv_done, n + 1)
                    dve.wait_ge(rinv_ready, n + 1)
                if heads[0] == 0 and u % 4 == 0 and not first:
                    dve.wait_ge(ot_done, 2 * g - 1 + u // 4)
                for e in heads:
                    h = slice(e * CH, (e + 1) * CH)
                    ins = dve.tensor_scalar(o_sb[h, u, :], o_bank(u, beside)[h, T + e * DH:T + (e + 1) * DH], rinv[h, u:u + 1],
                                            None, ALU.mult)
                if heads[-1] == 1:
                    ins.then_inc(o_ready, 1)

            def residual(g, beside=False):
                dve.wait_ge(wo_done, g + 1)
                dve.scalar_tensor_tensor(x1f[:, bass.DynSlice((g // B) * CH * B + g % B, CH, B)], bank[5 if beside else 7][:, 0:CH],
                                         cols[:, 1:2], xT[:, bass.ds((g % B) * T + (g // B) * CH, CH)], ALU.add, ALU.add).then_inc(x1_ready, 1)

            def unit_stages(g, u, first, before):
                scores(g, u, first)
                if u >= 1:
                    move_pt(g, u - 1, first)
                elif before:
                    move_pt(g - 1, PAIRS - 1, False)
                if u >= 2:
                    normalize(g, u - 2, first)
                elif before:
                    normalize(g - 1, PAIRS - 2 + u, False)
                if u == 4 and before:
                    residual(g - 1)

            x1f = x1T[:, :, :].rearrange("p t b -> p (t b)")
            for u in range(PAIRS):
                unit_stages(0, u, True, False)
            with dve.Fori(1, EARLY) as i:
                for u in range(PAIRS):
                    unit_stages(i, u, False, True)
            move_pt(EARLY - 1, PAIRS - 1, False)
            for u in (PAIRS - 2, PAIRS - 1):
                normalize(EARLY - 1, u, False)
            residual(EARLY - 1)

            def seed(block):
                cp(bank[block][:, 0:BLOCK * 2 * B].rearrange("p (t c) -> p t c", t=BLOCK),
                   vbias[:, 0:2, :].rearrange("p g b -> p (g b)").unsqueeze(1).broadcast_to([128, BLOCK, 2 * B]))
                cp(bank[2][:, block * BLOCK * B:(block + 1) * BLOCK * B].rearrange("p (t b) -> p t b", b=B),
                   vbias[:, 2:3, :].broadcast_to([128, BLOCK, B])).then_inc(seed_ok, 1)

            dve.wait_ge(gru_init, 5)
            dve.wait_ge(bits_set, 1)
            seed(0)

            def tile_stage(tau, step):
                m3 = mask[:, :].unsqueeze(2).broadcast_to([128, EXPERTS, HID])
                pre = lambda k: bank[k][:, :].rearrange("p (e n) -> p e n", e=EXPERTS)
                if step == 1:
                    dve.wait_ge(lg_done, tau + 1)
                    cp(lg[:, :], bank[3][:, 0:EXPERTS]).then_inc(lg_ok, 1)
                if step == 2:
                    dve.wait_ge(lg_ok, tau + 1)
                    dve.memset(pad[:, 2:3], 0.0)
                    dve.max(top[:, :], lg[:, :]).then_inc(top_ok, 1)
                if step == 3:
                    dve.wait_ge(top_ok, tau + 1)
                    dve.memset(pad[:, 3:4], 0.0)
                    dve.max_index(idx[:, :], top[:, :], lg[:, :]).then_inc(idx_ok, 1)
                if step == 4:
                    dve.wait_ge(idx_ok, tau + 1)
                    cp(idxf[:, :], idx[:, 0:1])
                    dve.wait_ge(rwt_ok, tau + 1)
                    dve.tensor_scalar(rw2[:, :], rw[:, :], 0.5, 0.5, ALU.mult, ALU.add).then_inc(idxf_ok, 1)
                    dve.wait_ge(idxf_ok, tau + 1)
                    dve.tensor_scalar(mask[:, :], iota[:, :], idxf[:, :], rw2[:, :], ALU.is_equal, ALU.mult).then_inc(mask_ok, 1)
                if step == 6:
                    dve.wait_ge(mask_ok, tau + 1)
                    dve.wait_ge(g_done, tau + 1)
                    dve.tensor_tensor(gm[:, :, :], pre(4), m3, ALU.mult).then_inc(gm_ok, 1)
                if step == 7:
                    dve.wait_ge(th_ok, tau + 1)
                    dve.scalar_tensor_tensor(sg[:, :, :], th[:, :, :], 1.0, gm[:, :, :], ALU.add, ALU.mult).then_inc(sg_ok, 1)
                if step == 8:
                    dve.wait_ge(u_done, tau + 1)
                    dve.tensor_tensor(um[:, :, :], pre(5), m3, ALU.mult).then_inc(um_ok, 1)
                if step == 9:
                    dve.wait_ge(sg_ok, tau + 1)
                    dve.wait_ge(um_ok, tau + 1)
                    dve.scalar_tensor_tensor(act_h[:, :, :], sg[:, :, :], 0.5, um[:, :, :], ALU.mult, ALU.mult).then_inc(ah_ok, 1)
                if step == 13:
                    dve.wait_ge(y_done, tau + 1)
                    if type(tau) is not int or tau > 0:
                        dve.wait_ge(stored, tau * 16)
                    cp(y_out[:, :], bank[6][:, 0:D]).then_inc(y_ok, 1)

            def window(i, k, groups, tiles, last):
                g = i + EARLY
                for lag in (5, 6, 3, 2):
                    for back in range(2):
                        if not groups[back][0] or not due(k, lag) or due(k, lag)[1] != back:
                            continue
                        u = due(k, lag)[0]
                        if lag == 2:
                            scores(g - back, u, False, True)
                        elif lag == 3:
                            dve.wait_ge(p_ready, (g - back) * PAIRS + u + 1)
                            invert(u)
                        else:
                            normalize(g - back, u, False, True, (lag - 5,))
                if groups[1][0] and k == 13:
                    residual(g - 1, True)
                for tau, step in tiles_at(i, k, tiles):
                    tile_stage(tau, step)
                if k == 1 or (k == 9 and not last):
                    seed(0 if k == 9 else 1)

            def period(i, groups, tiles, last):
                for k in range(PERIOD):
                    window(i, k, groups, tiles, last)
                    t = i * PERIOD + k
                    now, before = k % 2, 1 - k % 2
                    s = {n: a[:, now, 0:B] for n, a in st.items()}
                    tr, tz = trz[:, now, 0, :], trz[:, now, 1, :]
                    d8 = st["d8"][:, before, :]
                    stt = dve.scalar_tensor_tensor
                    dve.wait_ge(trz_ok, t + 1)
                    dve.wait_ge(d8_ok, t + 1)
                    stt(s["q8"], tr, 1.0, d8, ALU.add, ALU.mult).then_inc(q8_ok, 1)
                    stt(s["b1"], tz, -1.0, d8, ALU.add, ALU.mult).then_inc(b1_ok, 1)
                    stt(s["b8"], tz, -1.0, d8, ALU.add, ALU.mult).then_inc(b8_ok, 1)
                    dve.tensor_scalar(s["z8"], tz, 1.0, SPLIT, ALU.add, ALU.mult).then_inc(z8_ok, 1)
                    dve.wait_ge(b8_ok, t + 1)
                    dve.tensor_tensor(s["b2"], s["b8"], s["b1"], ALU.subtract).then_inc(b2_ok, 1)
                    dve.wait_ge(hh_ok, t + 1)
                    dve.wait_ge(z8_ok, t + 1)
                    dve.tensor_tensor(s["g1"], s["z8"], s["hh"], ALU.mult).then_inc(g1_ok, 1)
                    dve.tensor_tensor(s["g8"], s["z8"], s["hh"], ALU.mult).then_inc(g8_ok, 1)
                    dve.wait_ge(g8_ok, t + 1)
                    dve.tensor_tensor(s["g2"], s["g8"], s["g1"], ALU.subtract).then_inc(g2_ok, 1)
                    dve.wait_ge(hist_ok, t + 1)
                    stt(s["d8"], s["b8"], -0.5, s["g8"], ALU.mult, ALU.add).then_inc(d8_ok, 1)

            periods(dve, period)

            for step in range(TILE_STEPS):
                tile_stage(TILES - 1, step)


KQV = [("q", a, s) for a in range(PAIRS) for s in range(2)] + [("k", a, s) for a in range(PAIRS) for s in range(2)] \
    + [("v", a, s) for a in range(B * T // 128) for s in range(2)]
KQV_BANKS = 6
FIRST_E = tuple(range(19, 19 + 3 * PAIRS, 3))
KQV_ACT = (len(KQV) + 1) // 2
KQV_DVE = len(KQV) // 2
SETUP_ACT = 10
SETUP_DVE = 11


_INS = ['x', 'fside_Bx1x1024x16_0', 'cond_1024', 'L0_cond_W', 'L0_cond_fc_bias', 'L0_attn_Wq', 'L0_attn_Wkv', 'L0_attn_Wo',
        'L0_attn_bo', 'L0_attn_rel_emb', 'L0_cond2_W_z', 'L0_cond2_U_z', 'L0_cond2_C_z', 'L0_cond2_b_z', 'L0_cond2_W_r',
        'L0_cond2_U_r', 'L0_cond2_C_r', 'L0_cond2_b_r', 'L0_cond2_W', 'L0_cond2_U', 'L0_cond2_C', 'L0_cond2_b',
        'L0_ffn_gate_w', 'L0_ffn_w_gate', 'L0_ffn_w_up', 'L0_ffn_w_down']


def kernel(**inputs):
    import numpy as _np
    import concourse.bacc as _bacc
    from concourse import mybir as _mybir
    from concourse.bass_utils import run_bass_kernel_spmd as _run

    nc = _bacc.Bacc("TRN2", target_bir_lowering=False, num_devices=1)
    arrays, args = {}, []
    for name in _INS:
        a = _np.ascontiguousarray(inputs[name])
        arrays[f"in_{name}"] = a
        args.append(nc.dram_tensor(f"in_{name}", a.shape, _mybir.dt.from_np(a.dtype), kind="ExternalInput").ap())
    out = nc.dram_tensor("out", (B, T, D), _mybir.dt.float32, kind="ExternalOutput").ap()
    build(nc, *args, out)
    r = _run(nc, [arrays], core_ids=[0])
    return r.results[0]["out"]
```
